# Optimizing a Trainium2 kernel written in Bass

```python
import numpy as np
import jax
import jax.numpy as jnp

def _softmax(x, axis=-1):
    return jax.nn.softmax(x, axis=axis)

def _gelu(x):
    return jax.nn.gelu(x, approximate=True)

def _silu(x):
    return jax.nn.silu(x)

def _sigmoid(x):
    return jax.nn.sigmoid(x)

def _layernorm(x, axis=-1, eps=1e-05):
    m = jnp.mean(x, axis=axis, keepdims=True)
    v = jnp.var(x, axis=axis, keepdims=True)
    return (x - m) / jnp.sqrt(v + eps)

def _scatter_add(tgt, idx, src, axis=0):
    return tgt.at[idx].add(src)

def _segment_sum(src, seg, n):
    return jax.ops.segment_sum(src, seg, n)
kernel_name = 'mk_flamingo_gated_d4_seqx_r8_2d7bed'

def setup_inputs(seed: int=0):
    np.random.seed(seed)
    _w = jnp.asarray

    def _rec_inputs():
        import jax
        import jax.numpy as jnp
        _rk = jax.random.key(seed)
        x = 7.22e-05 + 1 * jax.random.normal(jax.random.fold_in(_rk, 1), (128, 64, 128), jnp.float32)
        _lenS = 64 - jax.random.randint(jax.random.fold_in(_rk, 7), (128,), 0, max(1, 64 // 4) + 1, jnp.int32)
        _lenS2 = 64 - jax.random.randint(jax.random.fold_in(_rk, 8), (128,), 0, max(1, 64 // 4) + 1, jnp.int32)
        _ctx_1024P = jax.random.normal(jax.random.fold_in(_rk, 11), (128, 16, 128), jnp.float32)
        _ctx_1024c = jax.random.dirichlet(jax.random.fold_in(_rk, 511), 0.3 * jnp.ones((16,), jnp.float32), (128, 64))
        _ctx_1024t = jnp.einsum('bsk,bkd->bsd', _ctx_1024c, _ctx_1024P)
        _ctx_1024t = _ctx_1024t * jax.lax.rsqrt(jnp.mean(jnp.square(_ctx_1024t)) + 1e-12) * 0.953939
        ctx_1024 = 4.13588e-05 + 0.999923 * (_ctx_1024t + 0.3 * jax.random.normal(jax.random.fold_in(_rk, 611), (128, 64, 128), jnp.float32))
        _validS = jnp.arange(64)[None, :] < _lenS[:, None]
        _validS2 = jnp.arange(64)[None, :] < _lenS2[:, None]
        _causal = jnp.tril(jnp.ones((64, 64), dtype=bool))
        mask_BxS2_bf0 = jnp.logical_not(jnp.ones((128, 64), dtype=bool))
        _g = jax.random.normal(jax.random.fold_in(_rk, 9001), (2, 4), jnp.float32)
        _g = jnp.sign(_g) * jnp.maximum(jnp.abs(_g), 1.0) + (_g == 0) * 1.0
        g_xattn = _g[0]
        g_ffn = _g[1]
        return (x, ctx_1024, mask_BxS2_bf0, g_xattn, g_ffn)
    x, ctx_1024, mask_BxS2_bf0, g_xattn, g_ffn = _rec_inputs()

    def _L0_xattn_setup():
        import jax, jax.numpy as jnp
        import numpy as np
        D_MODEL = 128
        HEADS = 16
        D_HEAD = D_MODEL // HEADS
        SEQ = 256
        C = 2
        K_TOP = int(C * np.log(SEQ))
        key = jax.random.key(seed)
        ks = jax.random.split(key, 5)
        s = 0.02
        return {'Q': jax.random.normal(ks[0], (4, SEQ, D_MODEL), jnp.float32), 'K': jax.random.normal(ks[1], (4, SEQ, D_MODEL), jnp.float32), 'V': jax.random.normal(ks[2], (4, SEQ, D_MODEL), jnp.float32), 'Wq': jax.random.normal(ks[3], (D_MODEL, D_HEAD), jnp.float32) * s, 'bq': jnp.zeros((D_HEAD,), jnp.float32), 'Wout': jax.random.normal(ks[4], (HEADS * D_HEAD, D_MODEL), jnp.float32) * s, 'bout': jnp.zeros((D_MODEL,), jnp.float32)}
    _L0_xattn_all = _L0_xattn_setup()
    _L0_xattn_in = {k: v for k, v in _L0_xattn_all.items() if k in ('Wq', 'bq', 'Wout', 'bout')}
    del _L0_xattn_all

    def _L0_ffn_setup():
        import jax, jax.numpy as jnp
        import numpy as np
        INT8_MAX = 127.0

        def _absmax_scale(x, axes):
            amax = jnp.max(jnp.abs(x), axis=axes, keepdims=True)
            return jnp.maximum(amax, 1e-12) / INT8_MAX
        key = jax.random.key(seed)
        k1, k2 = jax.random.split(key)
        lhs = jax.random.normal(k1, (4, 1024, 128), dtype=jnp.float32)
        rhs = jax.random.normal(k2, (128, 128), dtype=jnp.float32)
        return {'lhs': lhs, 'rhs': rhs}
    _L0_ffn_all = _L0_ffn_setup()
    _L0_ffn_in = {k: v for k, v in _L0_ffn_all.items() if k in ('rhs',)}
    del _L0_ffn_all

    def _L1_xattn_setup():
        import jax, jax.numpy as jnp
        import numpy as np
        EMBED_DIM = 128
        NUM_HEADS = 16
        HEAD_DIM = EMBED_DIM // NUM_HEADS
        B, T, S = (2, 256, 256)
        key = jax.random.key(seed)
        ks = jax.random.split(key, 12)
        xavier = lambda k: jax.random.uniform(k, (EMBED_DIM, EMBED_DIM), jnp.float32, -np.sqrt(6.0 / (2 * EMBED_DIM)), np.sqrt(6.0 / (2 * EMBED_DIM)))
        return {'query': jax.random.normal(ks[0], (B, T, EMBED_DIM), jnp.float32), 'key': jax.random.normal(ks[1], (B, S, EMBED_DIM), jnp.float32), 'value': jax.random.normal(ks[2], (B, S, EMBED_DIM), jnp.float32), 'key_padding_mask': jnp.zeros((B, S), dtype=bool), 'Wq': xavier(ks[3]), 'bq': jnp.zeros((EMBED_DIM,), jnp.float32), 'Wk': xavier(ks[4]), 'bk': jnp.zeros((EMBED_DIM,), jnp.float32), 'Wv': xavier(ks[5]), 'bv': jnp.zeros((EMBED_DIM,), jnp.float32), 'Wo': xavier(ks[6]), 'bo': jnp.zeros((EMBED_DIM,), jnp.float32)}
    _L1_xattn_all = _L1_xattn_setup()
    _L1_xattn_in = {k: v for k, v in _L1_xattn_all.items() if k in ('Wq', 'bq', 'Wk', 'bk', 'Wv', 'bv', 'Wo', 'bo')}
    del _L1_xattn_all

    def _L1_ffn_setup():
        import jax, jax.numpy as jnp
        import numpy as np
        EPS = 1e-08
        key = jax.random.key(seed)
        kx, kw = jax.random.split(key)
        x = jax.random.normal(kx, (8, 512, 128), dtype=jnp.float32)
        weight = jax.random.normal(kw, (128, 128), dtype=jnp.float32) * (1.0 / np.sqrt(128))
        return {'x': x, 'weight': weight}
    _L1_ffn_all = _L1_ffn_setup()
    _L1_ffn_in = {k: v for k, v in _L1_ffn_all.items() if k in ('weight',)}
    del _L1_ffn_all

    def _L2_xattn_setup():
        import jax, jax.numpy as jnp
        import numpy as np
        import math
        HIDDEN = 128
        HEADS = 16
        HEAD = HIDDEN // HEADS
        SCALE_BASE = 512.0

        def _gammas(heads):
            return 1.0 - jnp.exp(jnp.linspace(math.log(1.0 / 32.0), math.log(1.0 / 512.0), heads))

        def _xpos(x, downscale):
            S, d = (x.shape[2], x.shape[3])
            half = d // 2
            base_scale = (jnp.arange(0, d, 2, dtype=jnp.float32) + 0.4 * d) / (1.4 * d)
            pos = jnp.arange(S, dtype=jnp.float32)
            scale = base_scale[None, :] ** (pos / SCALE_BASE)[:, None]
            if downscale:
                scale = 1.0 / scale
            inv_freq = 1.0 / 10000.0 ** (jnp.arange(half, dtype=jnp.float32) / half)
            sinusoid = pos[:, None] * inv_freq[None, :]
            sin = jnp.repeat(jnp.sin(sinusoid) * scale, 2, axis=-1)
            cos = jnp.repeat(jnp.cos(sinusoid) * scale, 2, axis=-1)
            x1 = x[..., ::2]
            x2 = x[..., 1::2]
            rot = jnp.stack([-x2, x1], axis=-1).reshape(x.shape)
            return x * cos + rot * sin

        def _decay_mask(S, gammas):
            n = jnp.arange(S)[:, None]
            m = jnp.arange(S)[None, :]
            diff = (n - m).astype(jnp.float32)
            mask = n >= m
            pw = jnp.maximum(diff, 0.0)[None, :, :]
            return jnp.where(mask[None, :, :], gammas[:, None, None] ** pw, 0.0)

        def retention_forward(Q, K, V):
            B, S, _ = Q.shape

            def split(x, hd):
                return x.reshape(B, S, HEADS, hd).transpose(0, 2, 1, 3)
            q = _xpos(split(Q, HEAD), downscale=False)
            k = _xpos(split(K, HEAD), downscale=True)
            v = split(V, HEAD)
            D = _decay_mask(S, _gammas(HEADS).astype(Q.dtype))
            scores = jnp.einsum('bhsd,bhtd->bhst', q, k) * D[None]
            out = jnp.einsum('bhst,bhtd->bhsd', scores, v)
            return out.transpose(0, 2, 1, 3).reshape(B, S, HEADS * HEAD)
        key = jax.random.key(seed)
        kq, kk, kv = jax.random.split(key, 3)
        B, S = (2, 256)
        return {'Q': jax.random.normal(kq, (B, S, HIDDEN), dtype=jnp.float32), 'K': jax.random.normal(kk, (B, S, HIDDEN), dtype=jnp.float32), 'V': jax.random.normal(kv, (B, S, HIDDEN), dtype=jnp.float32)}
    _L2_xattn_all = _L2_xattn_setup()
    _L2_xattn_in = {k: v for k, v in _L2_xattn_all.items() if k in ()}
    del _L2_xattn_all

    def _L2_ffn_setup():
        import jax, jax.numpy as jnp
        import numpy as np
        HIDDEN = 128
        INNER = 512

        def _weight_quant(w):
            scale = 1.0 / jnp.clip(jnp.mean(jnp.abs(w)), 1e-05)
            wq = jnp.clip(jnp.round(w * scale), -1.0, 1.0) / scale
            return w + jax.lax.stop_gradient(wq - w)

        def _act_quant(x):
            scale = 127.0 / jnp.clip(jnp.max(jnp.abs(x), axis=-1, keepdims=True), 1e-05)
            xq = jnp.clip(jnp.round(x * scale), -128.0, 127.0) / scale
            return x + jax.lax.stop_gradient(xq - x)

        def _bitlinear(x, w):
            return jnp.einsum('bsi,oi->bso', _act_quant(x), _weight_quant(w))
        key = jax.random.key(seed)
        k0, k1, k2, k3 = jax.random.split(key, 4)
        x = jax.random.normal(k0, (4, 256, HIDDEN), dtype=jnp.float32)
        w_gate = jax.random.normal(k1, (INNER, HIDDEN), dtype=jnp.float32) / np.sqrt(HIDDEN)
        w_up = jax.random.normal(k2, (INNER, HIDDEN), dtype=jnp.float32) / np.sqrt(HIDDEN)
        w_down = jax.random.normal(k3, (HIDDEN, INNER), dtype=jnp.float32) / np.sqrt(INNER)
        return {'x': x, 'w_gate': w_gate, 'w_up': w_up, 'w_down': w_down}
    _L2_ffn_all = _L2_ffn_setup()
    _L2_ffn_in = {k: v for k, v in _L2_ffn_all.items() if k in ('w_gate', 'w_up', 'w_down')}
    del _L2_ffn_all

    def _L3_xattn_setup():
        import jax, jax.numpy as jnp
        import numpy as np
        import math
        D_MODEL = 128
        N_HEADS = 16
        HEAD_DIM = D_MODEL // N_HEADS

        def _split_heads(x, B, T):
            return x.reshape(B, T, N_HEADS, HEAD_DIM).transpose(0, 2, 1, 3)
        key = jax.random.key(seed)
        ks = jax.random.split(key, 11)
        B, T = (2, 256)
        s = 1.0 / math.sqrt(D_MODEL)
        return {'q': jax.random.normal(ks[0], (B, T, D_MODEL), jnp.float32), 'k': jax.random.normal(ks[1], (B, T, D_MODEL), jnp.float32), 'v': jax.random.normal(ks[2], (B, T, D_MODEL), jnp.float32), 'Wq': jax.random.normal(ks[3], (D_MODEL, D_MODEL), jnp.float32) * s, 'bq': jax.random.normal(ks[4], (D_MODEL,), jnp.float32) * s, 'Wk': jax.random.normal(ks[5], (D_MODEL, D_MODEL), jnp.float32) * s, 'bk': jax.random.normal(ks[6], (D_MODEL,), jnp.float32) * s, 'Wv': jax.random.normal(ks[7], (D_MODEL, D_MODEL), jnp.float32) * s, 'bv': jax.random.normal(ks[8], (D_MODEL,), jnp.float32) * s, 'Wo': jax.random.normal(ks[9], (D_MODEL, D_MODEL), jnp.float32) * s, 'bo': jax.random.normal(ks[10], (D_MODEL,), jnp.float32) * s}
    _L3_xattn_all = _L3_xattn_setup()
    _L3_xattn_in = {k: v for k, v in _L3_xattn_all.items() if k in ('Wq', 'bq', 'Wk', 'bk', 'Wv', 'bv', 'Wo', 'bo')}
    del _L3_xattn_all

    def _L3_ffn_setup():
        import jax, jax.numpy as jnp
        import numpy as np
        B, S, D = (2, 256, 128)
        H, E, P, K = (8, 8, 128, 2)
        SCALE = 1.0 / np.sqrt(P)

        def _get_sel_gate(x, w, route_scale):
            logits = jnp.einsum('bsd,ed->bse', x, w).astype(jnp.float32)
            raw = logits.reshape(x.shape[0], x.shape[1], H, E)
            probs = jax.nn.sigmoid(raw)
            vals, idx = jax.lax.top_k(probs, K)
            vals = vals / jnp.clip(vals.sum(-1, keepdims=True), 1e-09)
            vals = vals * route_scale
            gate = (jax.nn.one_hot(idx, E, dtype=vals.dtype) * vals[..., None]).sum(-2)
            return gate
        key = jax.random.key(seed)
        ks = jax.random.split(key, 8)
        std = 1.0 / np.sqrt(D)
        return {'x': jax.random.normal(ks[0], (B, S, D), jnp.float32), 'q_w': jax.random.normal(ks[1], (H * P, D), jnp.float32) * std, 'k_w': jax.random.normal(ks[2], (H * P, D), jnp.float32) * std, 'v_w': jax.random.normal(ks[3], (H * E, D, P), jnp.float32) * std, 'o_w': jax.random.normal(ks[4], (H * E, P, D), jnp.float32) * (1.0 / np.sqrt(H * P)), 'sel_v_w': jax.random.normal(ks[5], (H * E, D), jnp.float32) * std, 'sel_o_w': jax.random.normal(ks[6], (H * E, D), jnp.float32) * std, 'route_scale': jnp.ones((1,), jnp.float32)}
    _L3_ffn_all = _L3_ffn_setup()
    _L3_ffn_in = {k: v for k, v in _L3_ffn_all.items() if k in ('q_w', 'k_w', 'v_w', 'o_w', 'sel_v_w', 'sel_o_w', 'route_scale')}
    del _L3_ffn_all
    return {'x': x, 'ctx_1024': ctx_1024, 'mask_BxS2_bf0': mask_BxS2_bf0, 'g_xattn': g_xattn, 'g_ffn': g_ffn, 'L0_xattn_Wq': _L0_xattn_in['Wq'], 'L0_xattn_bq': _L0_xattn_in['bq'], 'L0_xattn_Wout': _L0_xattn_in['Wout'], 'L0_xattn_bout': _L0_xattn_in['bout'], 'L0_ffn_rhs': _L0_ffn_in['rhs'], 'L1_xattn_Wq': _L1_xattn_in['Wq'], 'L1_xattn_bq': _L1_xattn_in['bq'], 'L1_xattn_Wk': _L1_xattn_in['Wk'], 'L1_xattn_bk': _L1_xattn_in['bk'], 'L1_xattn_Wv': _L1_xattn_in['Wv'], 'L1_xattn_bv': _L1_xattn_in['bv'], 'L1_xattn_Wo': _L1_xattn_in['Wo'], 'L1_xattn_bo': _L1_xattn_in['bo'], 'L1_ffn_weight': _L1_ffn_in['weight'], 'L2_ffn_w_gate': _L2_ffn_in['w_gate'], 'L2_ffn_w_up': _L2_ffn_in['w_up'], 'L2_ffn_w_down': _L2_ffn_in['w_down'], 'L3_xattn_Wq': _L3_xattn_in['Wq'], 'L3_xattn_bq': _L3_xattn_in['bq'], 'L3_xattn_Wk': _L3_xattn_in['Wk'], 'L3_xattn_bk': _L3_xattn_in['bk'], 'L3_xattn_Wv': _L3_xattn_in['Wv'], 'L3_xattn_bv': _L3_xattn_in['bv'], 'L3_xattn_Wo': _L3_xattn_in['Wo'], 'L3_xattn_bo': _L3_xattn_in['bo'], 'L3_ffn_q_w': _L3_ffn_in['q_w'], 'L3_ffn_k_w': _L3_ffn_in['k_w'], 'L3_ffn_v_w': _L3_ffn_in['v_w'], 'L3_ffn_o_w': _L3_ffn_in['o_w'], 'L3_ffn_sel_v_w': _L3_ffn_in['sel_v_w'], 'L3_ffn_sel_o_w': _L3_ffn_in['sel_o_w'], 'L3_ffn_route_scale': _L3_ffn_in['route_scale']}

def reference(x, ctx_1024, mask_BxS2_bf0, g_xattn, g_ffn, L0_xattn_Wq, L0_xattn_bq, L0_xattn_Wout, L0_xattn_bout, L0_ffn_rhs, L1_xattn_Wq, L1_xattn_bq, L1_xattn_Wk, L1_xattn_bk, L1_xattn_Wv, L1_xattn_bv, L1_xattn_Wo, L1_xattn_bo, L1_ffn_weight, L2_ffn_w_gate, L2_ffn_w_up, L2_ffn_w_down, L3_xattn_Wq, L3_xattn_bq, L3_xattn_Wk, L3_xattn_bk, L3_xattn_Wv, L3_xattn_bv, L3_xattn_Wo, L3_xattn_bo, L3_ffn_q_w, L3_ffn_k_w, L3_ffn_v_w, L3_ffn_o_w, L3_ffn_sel_v_w, L3_ffn_sel_o_w, L3_ffn_route_scale):
    import jax
    import jax.numpy as jnp

    def _L0_xattn_ref(Q, K, V, Wq, bq, Wout, bout):
        import jax, jax.numpy as jnp
        import numpy as np
        D_MODEL = 128
        HEADS = 16
        D_HEAD = D_MODEL // HEADS
        SEQ = 256
        C = 2
        K_TOP = int(C * np.log(SEQ))
        B, L, _ = Q.shape
        q = (Q @ Wq + bq).transpose(0, 2, 1)
        k_ = (K @ Wq + bq).transpose(0, 2, 1)
        v = (V @ Wq + bq).transpose(0, 2, 1)
        Qf = jnp.fft.fft(q.astype(jnp.complex64))
        Kf = jnp.fft.fft(k_.astype(jnp.complex64))
        corr = jnp.real(jnp.fft.ifft(Qf * jnp.conj(Kf)))
        corr = corr.mean(axis=(0, 1))
        W_topk, I_topk = jax.lax.top_k(corr, K_TOP)
        W_topk = jax.nn.softmax(W_topk)

        def body(R, ws):
            w, shift = ws
            return (R + w * jnp.roll(v, -shift, axis=-1), None)
        R3, _ = jax.lax.scan(body, jnp.zeros_like(v), (W_topk, I_topk))
        R = jnp.broadcast_to(R3[:, None], (B, HEADS, D_HEAD, L)).reshape(B, L, HEADS * D_HEAD)
        return R @ Wout + bout

    def _L0_ffn_ref(lhs, rhs):
        import jax, jax.numpy as jnp
        import numpy as np
        INT8_MAX = 127.0

        def _absmax_scale(x, axes):
            amax = jnp.max(jnp.abs(x), axis=axes, keepdims=True)
            return jnp.maximum(amax, 1e-12) / INT8_MAX
        lhs_scale = _absmax_scale(lhs, (2,))
        rhs_scale = _absmax_scale(rhs, (0,))
        q_lhs = jnp.clip(jnp.round(lhs / lhs_scale), -INT8_MAX, INT8_MAX).astype(jnp.int8)
        q_rhs = jnp.clip(jnp.round(rhs / rhs_scale), -INT8_MAX, INT8_MAX).astype(jnp.int8)
        acc = jax.lax.dot_general(q_lhs, q_rhs, (((2,), (0,)), ((), ())), preferred_element_type=jnp.int32)
        return acc.astype(jnp.float32) * lhs_scale * rhs_scale

    def _L1_xattn_ref(query, key, value, key_padding_mask, Wq, bq, Wk, bk, Wv, bv, Wo, bo):
        import jax, jax.numpy as jnp
        import numpy as np
        EMBED_DIM = 128
        NUM_HEADS = 16
        HEAD_DIM = EMBED_DIM // NUM_HEADS
        B, T, S = (2, 256, 256)
        bsz, tgt_len, _ = query.shape
        src_len = key.shape[1]
        q = (query @ Wq.T + bq).reshape(bsz, tgt_len, NUM_HEADS, HEAD_DIM).transpose(0, 2, 1, 3)
        k = (key @ Wk.T + bk).reshape(bsz, src_len, NUM_HEADS, HEAD_DIM).transpose(0, 2, 1, 3)
        v = (value @ Wv.T + bv).reshape(bsz, src_len, NUM_HEADS, HEAD_DIM).transpose(0, 2, 1, 3)
        scale = HEAD_DIM ** (-0.5)
        scores = jnp.einsum('bhtd,bhsd->bhts', q, k) * scale
        causal_mask = jnp.triu(jnp.ones((tgt_len, src_len), dtype=bool), k=1)
        neg_inf = jnp.finfo(scores.dtype).min
        scores = jnp.where(causal_mask[None, None], neg_inf, scores)
        scores = jnp.where(key_padding_mask[:, None, None, :], neg_inf, scores)
        attn = jax.nn.softmax(scores, axis=-1)
        out = jnp.einsum('bhts,bhsd->bhtd', attn, v)
        out = out.transpose(0, 2, 1, 3).reshape(bsz, tgt_len, EMBED_DIM)
        return out @ Wo.T + bo

    def _L1_ffn_ref(x, weight):
        import jax, jax.numpy as jnp
        import numpy as np
        EPS = 1e-08
        w_scale = jnp.mean(jnp.abs(weight)) + EPS
        u = weight / w_scale
        w_quant = u + jax.lax.stop_gradient(jnp.clip(jnp.round(u), -1.0, 1.0) - u)
        a_scale = jnp.max(jnp.abs(x), axis=-1, keepdims=True) + EPS
        z = jnp.clip(x / a_scale * 127.0, -128.0, 127.0)
        a_quant = z + jax.lax.stop_gradient(jnp.round(z) - z)
        y = jnp.einsum('bsi,oi->bso', a_quant, w_quant)
        y = y * (w_scale * a_scale / 127.0)
        return y

    def _L2_xattn_ref(Q, K, V):
        import jax, jax.numpy as jnp
        import numpy as np
        import math
        HIDDEN = 128
        HEADS = 16
        HEAD = HIDDEN // HEADS
        SCALE_BASE = 512.0

        def _gammas(heads):
            return 1.0 - jnp.exp(jnp.linspace(math.log(1.0 / 32.0), math.log(1.0 / 512.0), heads))

        def _xpos(x, downscale):
            S, d = (x.shape[2], x.shape[3])
            half = d // 2
            base_scale = (jnp.arange(0, d, 2, dtype=jnp.float32) + 0.4 * d) / (1.4 * d)
            pos = jnp.arange(S, dtype=jnp.float32)
            scale = base_scale[None, :] ** (pos / SCALE_BASE)[:, None]
            if downscale:
                scale = 1.0 / scale
            inv_freq = 1.0 / 10000.0 ** (jnp.arange(half, dtype=jnp.float32) / half)
            sinusoid = pos[:, None] * inv_freq[None, :]
            sin = jnp.repeat(jnp.sin(sinusoid) * scale, 2, axis=-1)
            cos = jnp.repeat(jnp.cos(sinusoid) * scale, 2, axis=-1)
            x1 = x[..., ::2]
            x2 = x[..., 1::2]
            rot = jnp.stack([-x2, x1], axis=-1).reshape(x.shape)
            return x * cos + rot * sin

        def _decay_mask(S, gammas):
            n = jnp.arange(S)[:, None]
            m = jnp.arange(S)[None, :]
            diff = (n - m).astype(jnp.float32)
            mask = n >= m
            pw = jnp.maximum(diff, 0.0)[None, :, :]
            return jnp.where(mask[None, :, :], gammas[:, None, None] ** pw, 0.0)

        def retention_forward(Q, K, V):
            B, S, _ = Q.shape

            def split(x, hd):
                return x.reshape(B, S, HEADS, hd).transpose(0, 2, 1, 3)
            q = _xpos(split(Q, HEAD), downscale=False)
            k = _xpos(split(K, HEAD), downscale=True)
            v = split(V, HEAD)
            D = _decay_mask(S, _gammas(HEADS).astype(Q.dtype))
            scores = jnp.einsum('bhsd,bhtd->bhst', q, k) * D[None]
            out = jnp.einsum('bhst,bhtd->bhsd', scores, v)
            return out.transpose(0, 2, 1, 3).reshape(B, S, HEADS * HEAD)
        return retention_forward(Q, K, V)

    def _L2_ffn_ref(x, w_gate, w_up, w_down):
        import jax, jax.numpy as jnp
        import numpy as np
        HIDDEN = 128
        INNER = 512

        def _weight_quant(w):
            scale = 1.0 / jnp.clip(jnp.mean(jnp.abs(w)), 1e-05)
            wq = jnp.clip(jnp.round(w * scale), -1.0, 1.0) / scale
            return w + jax.lax.stop_gradient(wq - w)

        def _act_quant(x):
            scale = 127.0 / jnp.clip(jnp.max(jnp.abs(x), axis=-1, keepdims=True), 1e-05)
            xq = jnp.clip(jnp.round(x * scale), -128.0, 127.0) / scale
            return x + jax.lax.stop_gradient(xq - x)

        def _bitlinear(x, w):
            return jnp.einsum('bsi,oi->bso', _act_quant(x), _weight_quant(w))
        gate = jax.nn.silu(_bitlinear(x, w_gate))
        up = _bitlinear(x, w_up)
        return _bitlinear(gate * up, w_down)

    def _L3_xattn_ref(q, k, v, Wq, bq, Wk, bk, Wv, bv, Wo, bo):
        import jax, jax.numpy as jnp
        import numpy as np
        import math
        D_MODEL = 128
        N_HEADS = 16
        HEAD_DIM = D_MODEL // N_HEADS

        def _split_heads(x, B, T):
            return x.reshape(B, T, N_HEADS, HEAD_DIM).transpose(0, 2, 1, 3)
        B, Tq, _ = q.shape
        Tk = k.shape[1]
        qh = _split_heads(q @ Wq + bq, B, Tq)
        kh = _split_heads(k @ Wk + bk, B, Tk)
        vh = _split_heads(v @ Wv + bv, B, Tk)
        scale = 1.0 / math.sqrt(HEAD_DIM)
        scores = jnp.einsum('bhqd,bhkd->bhqk', qh, kh) * scale
        weights = jax.nn.softmax(scores, axis=-1)
        ctx = jnp.einsum('bhqk,bhkd->bhqd', weights, vh)
        ctx = ctx.transpose(0, 2, 1, 3).reshape(B, Tq, D_MODEL)
        return ctx @ Wo + bo

    def _L3_ffn_ref(x, q_w, k_w, v_w, o_w, sel_v_w, sel_o_w, route_scale):
        import jax, jax.numpy as jnp
        import numpy as np
        B, S, D = (2, 256, 128)
        H, E, P, K = (8, 8, 128, 2)
        SCALE = 1.0 / np.sqrt(P)

        def _get_sel_gate(x, w, route_scale):
            logits = jnp.einsum('bsd,ed->bse', x, w).astype(jnp.float32)
            raw = logits.reshape(x.shape[0], x.shape[1], H, E)
            probs = jax.nn.sigmoid(raw)
            vals, idx = jax.lax.top_k(probs, K)
            vals = vals / jnp.clip(vals.sum(-1, keepdims=True), 1e-09)
            vals = vals * route_scale
            gate = (jax.nn.one_hot(idx, E, dtype=vals.dtype) * vals[..., None]).sum(-2)
            return gate
        rs = route_scale[0]
        gate_v = _get_sel_gate(x, sel_v_w, rs)
        gate_o = _get_sel_gate(x, sel_o_w, rs)
        q = jnp.einsum('bsd,hpd->bhsp', x, q_w.reshape(H, P, D))
        k = jnp.einsum('bsd,hpd->bhsp', x, k_w.reshape(H, P, D))
        xv = jnp.einsum('bsd,hedp->bshep', x, v_w.reshape(H, E, D, P))
        v = jnp.einsum('bshep,bshe->bhsp', xv, gate_v)
        att = jax.nn.softmax(jnp.einsum('bhqp,bhkp->bhqk', q, k) * SCALE, axis=-1)
        ctx = jnp.einsum('bhqk,bhkp->bqhp', att, v)
        weighted = ctx[:, :, :, None, :] * gate_o[..., None]
        out = jnp.einsum('bshep,hepd->bsd', weighted, o_w.reshape(H, E, P, D))
        return out
    x = x + jnp.tanh(g_xattn[0]) * _L0_xattn_ref(_layernorm(x, axis=-1), ctx_1024, ctx_1024, L0_xattn_Wq, L0_xattn_bq, L0_xattn_Wout, L0_xattn_bout)
    x = x + jnp.tanh(g_ffn[0]) * _L0_ffn_ref(_layernorm(x, axis=-1), L0_ffn_rhs)
    x = x + jnp.tanh(g_xattn[1]) * _L1_xattn_ref(_layernorm(x, axis=-1), ctx_1024, ctx_1024, mask_BxS2_bf0, L1_xattn_Wq, L1_xattn_bq, L1_xattn_Wk, L1_xattn_bk, L1_xattn_Wv, L1_xattn_bv, L1_xattn_Wo, L1_xattn_bo)
    x = x + jnp.tanh(g_ffn[1]) * _L1_ffn_ref(_layernorm(x, axis=-1), L1_ffn_weight)
    x = x + jnp.tanh(g_xattn[2]) * _L2_xattn_ref(_layernorm(x, axis=-1), ctx_1024, ctx_1024)
    x = x + jnp.tanh(g_ffn[2]) * _L2_ffn_ref(_layernorm(x, axis=-1), L2_ffn_w_gate, L2_ffn_w_up, L2_ffn_w_down)
    x = x + jnp.tanh(g_xattn[3]) * _L3_xattn_ref(_layernorm(x, axis=-1), ctx_1024, ctx_1024, L3_xattn_Wq, L3_xattn_bq, L3_xattn_Wk, L3_xattn_bk, L3_xattn_Wv, L3_xattn_bv, L3_xattn_Wo, L3_xattn_bo)
    x = x + jnp.tanh(g_ffn[3]) * _L3_ffn_ref(_layernorm(x, axis=-1), L3_ffn_q_w, L3_ffn_k_w, L3_ffn_v_w, L3_ffn_o_w, L3_ffn_sel_v_w, L3_ffn_sel_o_w, L3_ffn_route_scale)
    return x

_drawn_inputs = setup_inputs


def setup_inputs(seed=0):
    import zlib

    import numpy as np

    out = dict(_drawn_inputs(seed))
    spreads = {'L0_xattn_bq': (0.0, 0.296),
     'L0_xattn_bout': (0.0, 0.1),
     'L1_xattn_bq': (0.0, 0.8),
     'L1_xattn_bk': (0.0, 0.8),
     'L1_xattn_bv': (0.0, 0.8),
     'L1_xattn_bo': (0.0, 0.717)}
    factors = {'g_ffn': 8.0,
     'L2_ffn_w_gate': 8.0,
     'L2_ffn_w_up': 8.0,
     'L2_ffn_w_down': 8.0,
     'L3_xattn_Wq': 7.519,
     'L3_xattn_bq': 8.0,
     'L3_xattn_Wk': 7.488,
     'L3_xattn_bk': 8.0,
     'L3_xattn_Wv': 2.987,
     'L3_xattn_bv': 8.0,
     'L3_xattn_Wo': 3.041,
     'L3_xattn_bo': 8.0,
     'L3_ffn_q_w': 8.0,
     'L3_ffn_k_w': 8.0,
     'L3_ffn_v_w': 8.0,
     'L3_ffn_o_w': 8.0,
     'L3_ffn_sel_v_w': 8.0,
     'L3_ffn_sel_o_w': 8.0}
    for name, (base, spread) in spreads.items():
        noise = np.random.default_rng([zlib.crc32(name.encode()), seed]).standard_normal(out[name].shape)
        drawn = base * np.exp(spread * noise) if base else spread * noise
        out[name] = jnp.asarray(drawn.astype(out[name].dtype))
    for name, factor in factors.items():
        out[name] = (out[name] * factor).astype(out[name].dtype)
    return out
```

```python
from contextlib import ExitStack, contextmanager

import numpy as np

import concourse.bass as bass
from concourse import mybir

ALU = mybir.AluOpType
ACT = mybir.ActivationFunctionType
F32 = mybir.dt.float32
F32R = mybir.dt.float32r
BF16 = mybir.dt.bfloat16
U8 = mybir.dt.uint8
AX = mybir.AxisListType

P = 128
B, S, D = 128, 64, 128
TILES = B * S // P
HEADS, HD = 16, 8
TOP_LAGS = int(2 * np.log(256))
C0 = 8
SH, SE = 8, 8
INNER = 512
EPS = 1e-5
ROUND = 12582912.0
NEG = -(2.0 ** 126)
FMIN = -3.0e38


def pipelined(eng, stages, unroll=2, tiles=TILES):
    depth = max(lag for lag, _ in stages)
    head = -(-(depth + unroll) // unroll)
    for t in range(head * unroll):
        for lag, step in stages:
            if t >= lag:
                step(t - lag, (t - lag) % unroll, (t - lag) // unroll)
    with eng.Fori(head, tiles // unroll) as r:
        for s in range(unroll):
            for lag, step in stages:
                step(r * unroll + (s - lag), (s - lag) % unroll, r + (s - lag) // unroll)
    for t in range(tiles, tiles + depth):
        for lag, step in stages:
            if 0 <= t - lag < tiles:
                step(t - lag, (t - lag) % unroll, (t - lag) // unroll)


def first(i, n):
    return isinstance(i, int) and i < n


def wait_alone(eng, *waits):
    if not all(isinstance(value, int) for _, value in waits):
        for _, value in waits:
            eng.lower_val(value)
        eng.wait_ge(waits[0][0], 1)
    for sem, value in waits:
        eng.wait_ge(sem, value)


def host_constants():
    p = np.arange(P)
    ident = np.eye(P, dtype=np.float32)
    half_heads = (p[:, None] % S // HD == np.arange(HEADS // 2)[None]).astype(np.float32)
    half_mask = (p[:, None] // S == np.arange(2)[None]).astype(np.float32)
    pos = (p % S).astype(np.float64)
    base = (np.arange(0, HD, 2) + 0.4 * HD) / (1.4 * HD)
    scale = base[None] ** (pos / 512.0)[:, None]
    freq = 1.0 / 10000.0 ** (np.arange(HD // 2) / (HD // 2))
    ang = pos[:, None] * freq[None]
    def spread(a):
        return np.tile(np.repeat(a, 2, axis=1), (1, HEADS))
    sign = np.tile(np.array([-1.0, 1.0]), D // 2)[None]
    rot = [spread(np.cos(ang) * scale), spread(np.sin(ang) * scale) * sign,
           spread(np.cos(ang) / scale), spread(np.sin(ang) / scale) * sign]
    gam = 1.0 - np.exp(np.linspace(np.log(1 / 32.0), np.log(1 / 512.0), HEADS))
    s, t = np.arange(S)[None, None], (p % S)[:, None, None]
    decay = np.where(s >= t, gam[None, :, None] ** np.maximum(s - t, 0), 0.0)
    causal = np.where(np.arange(S)[None] > (p % S)[:, None], NEG, 0.0)
    place = (8 - np.arange(SE)).astype(np.float32)
    c = dict(ident=ident, half_heads=half_heads, half_mask=half_mask, rot=np.concatenate(rot, 1),
             decay=decay.reshape(P, HEADS * S), causal=causal,
             place=np.broadcast_to(np.tile(place, 2 * SH), (P, 2 * SH * SE)))
    return {k: np.ascontiguousarray(v, dtype=np.float32) for k, v in c.items()}


class Core:

    def __init__(self, nc):
        self.nc = nc
        self.stack = ExitStack()
        self.scope_sems = []

    @contextmanager
    def scope(self):
        outer, self.stack = self.stack, ExitStack()
        outer_sems, self.scope_sems = self.scope_sems, []
        try:
            with self.stack:
                yield
                if self.scope_sems:
                    self.nc.clear_and_free_semaphores(self.scope_sems)
                    self.nc.all_engine_barrier()
        finally:
            self.stack, self.scope_sems = outer, outer_sems

    def sb(self, name, shape, dt=F32):
        return self.stack.enter_context(self.nc.sbuf_tensor(name, list(shape), dt))

    def psum(self, name, shape, dt=F32):
        bank = 1024 if dt == BF16 else 512
        size = int(np.prod(shape[1:]))
        t = self.stack.enter_context(self.nc.psum_tensor("ps_" + name, [P, -(-size // bank) * bank], dt))
        view = t[0:shape[0], 0:size]
        if len(shape) == 3:
            view = view.rearrange("p (a b) -> p a b", a=shape[1])
        if len(shape) == 4:
            view = view.rearrange("p (a b c) -> p a b c", a=shape[1], b=shape[2])
        return view

    def sem(self, name):
        self.scope_sems.append(self.nc.alloc_semaphore(name=name))
        return self.scope_sems[-1]

    def sems(self, prefix, *names):
        return {n: self.sem(f"{prefix}_{n}") for n in names}


def col(ap1d):
    return ap1d.rearrange("(p a) -> p a", a=1)


def on_all(ap1d, n):
    return ap1d.rearrange("(a n) -> a n", a=1).broadcast_to([P, n])


def tile_of(buf, i):
    return buf[:, bass.ds(i, 1), :].rearrange("p a d -> p (a d)")


def build_constants(k, A, C):
    nc = k.nc
    for name, shape in (("ident", [P, P]), ("half_heads", [P, HEADS // 2]), ("half_mask", [P, 2])):
        C[name] = k.sb("c_" + name, shape)
    C["gates"] = k.sb("gates", [P, 8])
    C["ones"] = k.sb("ones", [P, P])
    C["ident16"] = k.sb("ident16", [P, P], BF16)
    C["minus_half"] = k.sb("minus_half", [P, 1])
    raw = k.sb("gates_raw", [P, 8])
    q = k.sems("c", "loaded", "tanh", "set")
    with nc.Block() as block:
        @block.sync
        def _(sp):
            for name in ("ident", "half_heads", "half_mask"):
                sp.dma_start(C[name][:], A["c_" + name]).then_inc(q["loaded"], 16)
            sp.dma_start(raw[:, 0:4], on_all(A["g_xattn"], 4)).then_inc(q["loaded"], 16)
            sp.dma_start(raw[:, 4:8], on_all(A["g_ffn"], 4)).then_inc(q["loaded"], 16)

        @block.scalar
        def _(act):
            act.wait_ge(q["loaded"], 80)
            act.activation(C["gates"][:], raw[:], ACT.Tanh).then_inc(q["tanh"], 1)

        @block.vector
        def _(dve):
            dve.memset(C["ones"][:], 1.0).then_inc(q["set"], 1)
            dve.memset(C["minus_half"][:], -0.5).then_inc(q["set"], 1)
            dve.wait_ge(q["loaded"], 80)
            dve.tensor_copy(C["ident16"][:], C["ident"][:]).then_inc(q["set"], 1)


def turn(k, prefix, pairs, ident, dt, scales=None):
    nc = k.nc
    with k.scope():
        ps = [k.psum(f"{prefix}_ps{n}", [P, P], dt) for n in range(2)]
        q = k.sems(prefix, "turned", "kept")
        with nc.Block() as block:
            @block.tensor
            def _(pe):
                for n, (_, src) in enumerate(pairs):
                    if n >= 2:
                        pe.wait_ge(q["kept"], n - 1)
                    pe.transpose(ps[n % 2][:], src, ident).then_inc(q["turned"], 1)

            @block.vector
            def _(dve):
                for n, (dst, _) in enumerate(pairs):
                    dve.wait_ge(q["turned"], n + 1)
                    dve.tensor_copy(dst, ps[n % 2][:]).then_inc(q["kept"], 1)



LN_SEMS = ("stats", "moments", "var_eps", "rstd", "xhat")


def ln_buffers(k, name, unroll=2):
    return dict(stats=k.sb(name + "_stats", [P, unroll, 6]), mv=k.sb(name + "_mv", [P, unroll, 2]),
                var=k.sb(name + "_var", [P, unroll]), rstd=k.sb(name + "_rstd", [P, unroll]),
                xhat=k.sb(name + "_xhat", [P, unroll, P]))


def ln_moments(dve, q, L, x_i, i, s, ready):
    if ready is not None:
        wait_alone(dve, ready)
    dve.bn_stats(L["stats"][:, s], x_i).then_inc(q["stats"], 1)
    wait_alone(dve, (q["stats"], i + 1))
    dve.bn_aggr(L["mv"][:, s], L["stats"][:, s]).then_inc(q["moments"], 1)
    dve.wait_ge(q["moments"], i + 1)
    dve.tensor_scalar(L["var"][:, s:s + 1], L["mv"][:, s, 1:2], EPS, None, ALU.add).then_inc(q["var_eps"], 1)


def ln_rstd(pool, q, L, half, i, s, unroll=2):
    pool.wait_ge(q["var_eps"], i + 1)
    if not first(i, unroll):
        pool.wait_ge(q["xhat"], i - unroll + 1)
    pool.tensor_tensor(L["rstd"][:, s:s + 1], L["var"][:, s:s + 1], half, ALU.pow).then_inc(q["rstd"], 1)


def ln_xhat(dve, q, L, x_i, i, s, reader=None, unroll=2):
    dve.wait_ge(q["rstd"], i + 1)
    if reader is not None and not first(i, unroll):
        dve.wait_ge(reader, i - unroll + 1)
    dve.tensor_scalar(L["xhat"][:, s], x_i, L["mv"][:, s, 0:1], L["rstd"][:, s:s + 1],
                      ALU.subtract, ALU.mult).then_inc(q["xhat"], 1)



def load_and_correlate(k, A, C, X, CT, V0):
    nc = k.nc
    GT = k.sb("GT", [S, 2, S])
    with k.scope():
        NS = 4
        L = ln_buffers(k, "l0", NS)
        ctx = k.sb("l0_ctx", [P, NS, P])
        xT = k.sb("l0_xT", [P, NS, P])
        wq = k.sb("l0_wq", [P, C0])
        bq_col = k.sb("l0_bq_col", [C0, 1])
        qk = k.sb("l0_qk", [C0, NS, 2 * P])
        ps_turn = [k.psum(f"l0_turn{n}", [P, 2, P]) for n in range(2)]
        ps_qk = [k.psum(f"l0_qkp{n}", [P, 2 * P]) for n in range(2)]
        ps_v = [k.psum(f"l0_v{n}", [P, C0]) for n in range(2)]
        ps_g = k.psum("l0_g", [S, S])
        q = k.sems("l0", "weights", *LN_SEMS, "turned", "xT", "ctxT", "qk_ps", "v_ps", "qk", "v", "summed", "g")
        loaded = [k.sem(f"l0_loaded{n}") for n in range(NS)]
        with nc.Block() as block:
            @block.sync
            def _(sp):
                sp.dma_start(wq[:], A["L0_xattn_Wq"]).then_inc(q["weights"], 16)
                sp.dma_start(bq_col[:], col(A["L0_xattn_bq"])).then_inc(q["weights"], 16)

                def load(i, s, r):
                    if not first(i, NS):
                        sp.wait_ge(q["turned"], i - NS + 1)
                    sp.dma_start(tile_of(X, i), A["x_tiles"][bass.ds(i, 1)].rearrange("a p d -> (a p) d"))\
                        .then_inc(loaded[s], 16)
                    sp.dma_start(ctx[:, s], A["ctx_tiles"][bass.ds(i, 1)].rearrange("a p d -> (a p) d"))\
                        .then_inc(loaded[s], 16)
                pipelined(sp, [(0, load)], NS)

            @block.gpsimd
            def _(pool):
                pipelined(pool, [(0, lambda i, s, r: ln_rstd(pool, q, L, C["minus_half"][:], i, s, NS))], NS)

            @block.vector
            def _(dve):
                def front(i, s, r):
                    ln_moments(dve, q, L, tile_of(X, i), i, s, (loaded[s], 32 * r + 32))

                def norm(i, s, r):
                    ln_xhat(dve, q, L, tile_of(X, i), i, s, q["turned"], NS)

                def keep_ctx(i, s, r):
                    dve.wait_ge(q["turned"], i + 1)
                    dve.wait_ge(q["xT"], i + 1)
                    dve.tensor_copy(tile_of(CT, i), ps_turn[s % 2][:, 1]).then_inc(q["ctxT"], 1)

                def keep_v(i, s, r):
                    dve.wait_ge(q["v_ps"], i + 1)
                    dve.tensor_copy(tile_of(V0, i), ps_v[s % 2][:]).then_inc(q["v"], 1)
                pipelined(dve, [(0, front), (1, norm), (2, keep_ctx), (3, keep_v)], NS)
                dve.wait_ge(q["summed"], TILES)
                dve.tensor_copy(GT[:, 0], ps_g[:]).then_inc(q["g"], 1)
                dve.tensor_copy(GT[:, 1], ps_g[:]).then_inc(q["g"], 1)

            @block.scalar
            def _(act):
                act.preload_act_table(ACT.Exp)
                act.wait_ge(q["weights"], 32)

                def keep_x(i, s, r):
                    act.wait_ge(q["turned"], i + 1)
                    if not first(i, NS):
                        act.wait_ge(q["qk_ps"], i - NS + 1)
                    act.activation(xT[:, s], ps_turn[s % 2][:, 0], ACT.Copy).then_inc(q["xT"], 1)

                def keep_qk(i, s, r):
                    act.wait_ge(q["qk_ps"], i + 1)
                    if not first(i, NS):
                        act.wait_ge(q["summed"], i - NS + 1)
                    act.activation(qk[:, s], ps_qk[s % 2][0:C0], ACT.Identity, bias=bq_col[:]).then_inc(q["qk"], 1)
                pipelined(act, [(0, keep_x), (1, keep_qk)], NS)

            @block.tensor
            def _(pe):
                pe.wait_ge(q["weights"], 32)

                def turns(i, s, r):
                    pe.wait_ge(q["xhat"], i + 1)
                    pe.wait_ge(loaded[s], 32 * r + 32)
                    if not first(i, 2):
                        pe.wait_ge(q["ctxT"], i - 1)
                    pe.transpose(ps_turn[s % 2][:, 0], L["xhat"][:, s], C["ident"][:])
                    pe.transpose(ps_turn[s % 2][:, 1], ctx[:, s], C["ident"][:]).then_inc(q["turned"], 1)

                def project(i, s, r):
                    pe.wait_ge(q["xT"], i + 1)
                    pe.wait_ge(q["ctxT"], i + 1)
                    if not first(i, 2):
                        pe.wait_ge(q["qk"], i - 1)
                    pe.matmul(ps_qk[s % 2][0:C0, 0:P], wq[:], xT[:, s], start=True, stop=True)
                    pe.matmul(ps_qk[s % 2][0:C0, P:2 * P], wq[:], tile_of(CT, i), start=True, stop=True)\
                        .then_inc(q["qk_ps"], 1)

                def sum_pairs(i, s, r):
                    read = [] if first(i, 2) else [(q["v"], i - 1)]
                    wait_alone(pe, (q["qk"], i + 1), *read)
                    pe.transpose(ps_v[s % 2][:], qk[:, s, P:2 * P], C["ident"][0:C0, 0:C0]).then_inc(q["v_ps"], 1)
                    for h in range(2):
                        g = pe.matmul(ps_g[:], qk[:, s, P + h * S:P + (h + 1) * S], qk[:, s, h * S:(h + 1) * S],
                                      start=first(i, 1) and h == 0,
                                      stop=isinstance(i, int) and i == TILES - 1 and h == 1,
                                      skip_group_check=True)
                    g.then_inc(q["summed"], 1)
                pipelined(pe, [(0, turns), (1, project), (2, sum_pairs)], NS)
    return GT


def lag_weights(k, A, C, GT, OUT0, V0, scratch):
    nc = k.nc
    with k.scope():
        lags = k.sb("lag_skewed", [S, S])
        corr = k.sb("lag_corr", [P, S])
        left1 = k.sb("lag_left1", [P, S])
        left2 = k.sb("lag_left2", [P, S])
        top = k.sb("lag_top", [P, 2, 8])
        chosen = k.sb("lag_chosen", [P, S])
        small = k.sb("lag_small", [P, 4])
        w2 = k.sb("lag_w2", [P, 2, S])
        circ = k.sb("lag_circ", [P, 2, S])
        wout = k.sb("lag_wout", [P, D])
        bout = k.sb("lag_bout", [D, 1])
        MAX_KNOWN, WEIGHTS_TWICE, WEFF_KEPT = 8, 13, 15
        weff = k.sb("lag_weff", [P, 2, D])
        ps_c = k.psum("lag_c", [P, S])
        ps_w = [k.psum(f"lag_w{n}", [P, D]) for n in range(2)]
        ps_o = [k.psum(f"lag_o{n}", [P, TILES, 4]) for n in range(2)]
        q = k.sems("lag", "stored", "skewed", "corr_ps", "d", "exp", "w_stored", "circ", "wout", "weff_ps", "out_ps")
        GW, CW = 2 * S, 4 * S
        g_rows, w_rows = scratch["lags"], scratch["circ"]
        with nc.Block() as block:
            @block.sync
            def _(sp):
                sp.dma_start(wout[:], A["L0_xattn_Wout"]).then_inc(q["wout"], 16)
                sp.dma_start(bout[:], col(A["L0_xattn_bout"])).then_inc(q["wout"], 16)
                sp.dma_start(bass.AP(g_rows, 0, [[GW, S], [1, GW]]), GT[:].rearrange("p a b -> p (a b)"))\
                    .then_inc(q["stored"], 16)
                sp.wait_ge(q["stored"], 16)
                sp.dma_start(lags[:], bass.AP(g_rows, 0, [[GW + 1, S], [1, S]])).then_inc(q["skewed"], 16)
                sp.wait_ge(q["d"], WEIGHTS_TWICE)
                sp.dma_start(bass.AP(w_rows, 0, [[CW + 1, S], [1, 2 * S]]), w2[0:S].rearrange("p a b -> p (a b)"))\
                    .then_inc(q["w_stored"], 16)
                sp.wait_ge(q["w_stored"], 16)
                for half in range(2):
                    for copy in range(2):
                        sp.dma_start(circ[half * S:(half + 1) * S, copy], bass.AP(w_rows, S, [[CW, S], [1, S]]))\
                            .then_inc(q["circ"], 16)

            @block.tensor
            def _(pe):
                pe.wait_ge(q["skewed"], 16)
                pe.matmul(ps_c, C["ones"][0:S], lags[:], start=True, stop=True).then_inc(q["corr_ps"], 1)
                pe.wait_ge(q["circ"], 64)
                pe.wait_ge(q["wout"], 32)
                for cp in range(2):
                    h = slice(cp * S, (cp + 1) * S)
                    m = pe.matmul(ps_w[cp], circ[h].rearrange("p a b -> p (a b)"), wout[h],
                                  start=True, stop=True)
                    m.then_inc(q["weff_ps"], 1)
                pe.wait_ge(q["d"], WEFF_KEPT)
                for half in range(2):
                    h = slice(half * S, (half + 1) * S)
                    for cp in range(2):
                        v = V0[h].rearrange("p t (r c) -> p t r c", c=2)[:, :, :, cp]
                        m = pe.matmul(ps_o[half], weff[h, cp], v, start=cp == 0, stop=cp == 1)
                    m.then_inc(q["out_ps"], 1)

            @block.scalar
            def _(act):
                act.preload_act_table(ACT.Exp)
                act.wait_ge(q["d"], MAX_KNOWN)
                act.activation(w2[:, 1], corr[:], ACT.Exp, bias=small[:, 0:1]).then_inc(q["exp"], 1)

            @block.vector
            def _(dve):
                done = [0]

                def link(ins):
                    done[0] += 1
                    ins.then_inc(q["d"], 1)
                    dve.wait_ge(q["d"], done[0])

                dve.wait_ge(q["wout"], 32)
                dve.wait_ge(q["corr_ps"], 1)
                link(dve.tensor_scalar(corr[:], ps_c, 1.0 / (B * C0), None, ALU.mult))
                link(dve.max(top[:, 0], corr[:]))
                link(dve.match_replace(left1[:], top[:, 0], corr[:], FMIN))
                link(dve.max(top[:, 1], left1[:]))
                link(dve.memset(top[:, 1, TOP_LAGS - 8:8], FMIN))
                link(dve.match_replace(left2[:], top[:, 1], left1[:], FMIN))
                link(dve.tensor_scalar(chosen[:], left2[:], FMIN, None, ALU.is_equal))
                link(dve.tensor_scalar(small[:, 0:1], top[:, 0, 0:1], -1.0, None, ALU.mult))
                assert done[0] == MAX_KNOWN
                dve.wait_ge(q["exp"], 1)
                link(dve.tensor_tensor(w2[:, 0], w2[:, 1], chosen[:], ALU.mult))
                link(dve.tensor_reduce(small[:, 1:2], w2[:, 0], AX.X, ALU.add))
                link(dve.reciprocal(small[:, 2:3], small[:, 1:2]))
                link(dve.tensor_scalar(w2[:, 1], w2[:, 0], small[:, 2:3], None, ALU.mult))
                link(dve.tensor_copy(w2[:, 0], w2[:, 1]))
                assert done[0] == WEIGHTS_TWICE
                dve.wait_ge(q["weff_ps"], 2)
                for cp in range(2):
                    link(dve.tensor_copy(weff[:, cp], ps_w[cp]))
                assert done[0] == WEFF_KEPT
                for half in range(2):
                    dve.wait_ge(q["out_ps"], half + 1)
                    link(dve.tensor_scalar(OUT0[:, half], ps_o[half], bout[:], C["gates"][:, 0:1],
                                           ALU.add, ALU.mult))



def prepare_quantised(k, A, W):
    nc = k.nc
    W["ff0"] = k.sb("w_ff0", [P, D], BF16)
    W["ff0_scale"] = k.sb("w_ff0_scale", [P, D])
    W["ff1"] = k.sb("w_ff1", [P, D], BF16)
    W["gate_up"] = k.sb("w_gate_up", [P, 2 * INNER], BF16)
    W["down"] = k.sb("w_down", [P, INNER // P, D], BF16)
    W["means"] = k.sb("w_means", [P, 4])
    W["ff1_out"] = k.sb("w_ff1_out", [P, 1])
    W["down_out"] = k.sb("w_down_out", [P, 1])
    C = W["C"]
    NB = 1 + 4 + 4 + 4
    with k.scope():
        raw = k.sb("pq_raw", [P, NB, P])
        shifted = k.sb("pq_shifted", [P, NB, P])
        quant = k.sb("pq_quant", [P, NB, P], BF16)
        sums = k.sb("pq_sums", [P, 4])
        inv = k.sb("pq_inv", [P, 4])
        rhs = k.sb("pq_rhs", [P, P])
        rhs_T = k.sb("pq_rhs_T", [P, P])
        rhs_q = k.sb("pq_rhs_q", [P, P], BF16)
        diag = k.sb("pq_diag", [P, P])
        amax = k.sb("pq_amax", [P, 3])
        ps_s = k.psum("pq_sum", [P, 4])
        ps_r = k.psum("pq_rhs", [P, P])
        ps_b = k.psum("pq_bcast", [P, P])
        q = k.sems("pq", "loaded", "d", "sum_ps", "rhs_ps", "scale_ps")
        blocks = [slice(0, 1), slice(1, 5), slice(5, 9), slice(9, 13)]
        SUMMED, DIAG = 4, 9
        with nc.Block() as block:
            @block.sync
            def _(sp):
                sp.dma_start(raw[:, 0], A["L1_ffn_weight"]).then_inc(q["loaded"], 16)
                for n, name in ((1, "L2_ffn_w_gate"), (5, "L2_ffn_w_up")):
                    sp.dma_start(raw[:, n:n + 4], A[name].rearrange("(a p) i -> p a i", p=P)).then_inc(q["loaded"], 16)
                sp.dma_start(raw[:, 9:13], A["L2_ffn_w_down"].rearrange("o (a j) -> o a j", j=P)).then_inc(q["loaded"], 16)
                sp.dma_start(rhs[:], A["L0_ffn_rhs"]).then_inc(q["loaded"], 16)

            @block.tensor
            def _(pe):
                pe.wait_ge(q["loaded"], 80)
                pe.transpose(ps_r, rhs[:], C["ident"][:]).then_inc(q["rhs_ps"], 1)
                pe.wait_ge(q["d"], SUMMED)
                pe.matmul(ps_s, C["ones"][:], sums[:], start=True, stop=True).then_inc(q["sum_ps"], 1)
                pe.wait_ge(q["d"], DIAG)
                pe.matmul(ps_b, C["ones"][:], diag[:], start=True, stop=True).then_inc(q["scale_ps"], 1)

            @block.vector
            def _(dve):
                done = [0]

                def link(ins):
                    done[0] += 1
                    ins.then_inc(q["d"], 1)
                    dve.wait_ge(q["d"], done[0])

                dve.wait_ge(q["loaded"], 80)
                for n, b in enumerate(blocks):
                    link(dve.tensor_reduce(sums[:, n:n + 1], raw[:, b], AX.XY, ALU.add, apply_absolute_value=True))
                assert done[0] == SUMMED
                dve.wait_ge(q["rhs_ps"], 1)
                link(dve.tensor_copy(rhs_T[:], ps_r))
                link(dve.tensor_reduce(amax[:, 0:1], rhs_T[:], AX.X, ALU.max, apply_absolute_value=True))
                link(dve.tensor_scalar(amax[:, 1:2], amax[:, 0:1], 1e-12, 1.0 / 127.0, ALU.max, ALU.mult))
                link(dve.reciprocal(amax[:, 2:3], amax[:, 1:2]))
                link(dve.tensor_scalar(diag[:], C["ident"][:], amax[:, 1:2], C["gates"][:, 4:5], ALU.mult, ALU.mult))
                assert done[0] == DIAG
                link(dve.tensor_scalar(rhs_T[:], rhs_T[:], amax[:, 2:3], 127.0, ALU.mult, ALU.min))
                link(dve.tensor_scalar(rhs_T[:], rhs_T[:], -127.0, ROUND, ALU.max, ALU.add))
                link(dve.tensor_scalar(rhs_q[:], rhs_T[:], ROUND, None, ALU.subtract))
                dve.wait_ge(q["scale_ps"], 1)
                link(dve.tensor_copy(W["ff0_scale"][:], ps_b))
                dve.wait_ge(q["sum_ps"], 1)
                link(dve.tensor_scalar(W["means"][:, 0:1], ps_s[:, 0:1], 1.0 / (D * D), 1e-8, ALU.mult, ALU.add))
                link(dve.tensor_scalar(W["means"][:, 1:4], ps_s[:, 1:4], 1.0 / (D * INNER), 1e-5, ALU.mult, ALU.max))
                link(dve.reciprocal(inv[:], W["means"][:]))
                link(dve.tensor_tensor(W["ff1_out"][:], W["means"][:, 0:1], C["gates"][:, 5:6], ALU.mult))
                link(dve.tensor_tensor(W["down_out"][:], W["means"][:, 3:4], C["gates"][:, 6:7], ALU.mult))
                for n, b in enumerate(blocks):
                    link(dve.tensor_scalar(shifted[:, b], raw[:, b], inv[:, n:n + 1], ROUND, ALU.mult, ALU.add))
                link(dve.tensor_scalar(shifted[:], shifted[:], ROUND, 1.0, ALU.subtract, ALU.min))
                link(dve.tensor_scalar(quant[:], shifted[:], -1.0, None, ALU.max))
        pairs = [(W["ff0"][:], rhs_q[:]), (W["ff1"][:], quant[:, 0])]
        pairs += [(W["gate_up"][:, n * P:(n + 1) * P], quant[:, 1 + n]) for n in range(8)]
        pairs += [(W["down"][:, n], quant[:, 9 + n]) for n in range(4)]
        turn(k, "pq_turn", pairs, C["ident16"][:], BF16)


QUANT_SEMS = ("absmax", "scale", "inverse", "clipped", "shifted", "rounded")


def quantise(dve, q, Qb, src, floor, i, s):
    op, eps = floor
    dve.tensor_reduce(Qb["amax"][:, s:s + 1], src, AX.X, ALU.max, apply_absolute_value=True)\
        .then_inc(q["absmax"], 1)
    dve.wait_ge(q["absmax"], i + 1)
    dve.tensor_scalar(Qb["scale"][:, s:s + 1], Qb["amax"][:, s:s + 1], eps, 1.0 / 127.0, op, ALU.mult)\
        .then_inc(q["scale"], 1)
    dve.wait_ge(q["scale"], i + 1)
    dve.reciprocal(Qb["inv"][:, s:s + 1], Qb["scale"][:, s:s + 1]).then_inc(q["inverse"], 1)
    dve.wait_ge(q["inverse"], i + 1)
    dve.tensor_scalar(Qb["clipped"][:, s], src, Qb["inv"][:, s:s + 1], 127.0, ALU.mult, ALU.min)\
        .then_inc(q["clipped"], 1)
    dve.wait_ge(q["clipped"], i + 1)
    if not first(i, 4):
        dve.wait_ge(q["rounded"], i - 3)
    dve.tensor_scalar(Qb["shifted"][:, s], Qb["clipped"][:, s], -127.0, ROUND, ALU.max, ALU.add)\
        .then_inc(q["shifted"], 1)


def quantise_buffers(k, name, width):
    return dict(amax=k.sb(name + "_amax", [P, 4]), scale=k.sb(name + "_scale", [P, 4]),
                inv=k.sb(name + "_inv", [P, 4]), clipped=k.sb(name + "_clipped", [P, 4, width]),
                shifted=k.sb(name + "_shifted", [P, 4, width]), q16=k.sb(name + "_q16", [P, 4, width], BF16))


def feed_forward_int(k, A, C, W, X, layer, OUT0):
    nc = k.nc
    w16 = W["ff0"] if layer == 0 else W["ff1"]
    floor = (ALU.max, 1e-12) if layer == 0 else (ALU.add, 1e-8)
    with k.scope():
        name = f"ff{layer}"
        L = ln_buffers(k, name, 4)
        Qb = quantise_buffers(k, name, P)
        rows = k.sb(name + "_rows", [P, 4, P])
        qT = k.sb(name + "_qT", [P, 4, P], BF16)
        out_scale = k.sb(name + "_out_scale", [P, 4])
        scaled = k.sb(name + "_scaled", [P, 4, P])
        ps_rows = [k.psum(f"{name}_rows{n}", [P, P]) for n in range(2)]
        ps_q = [k.psum(f"{name}_q{n}", [P, P], BF16) for n in range(2)]
        ps_y = [k.psum(f"{name}_y{n}", [P, P]) for n in range(2)]
        q = k.sems(name, *LN_SEMS, *QUANT_SEMS, "rows", "rows_ps", "added", "turned", "qT", "y", "out_scale",
                   "scaled", "x")
        with nc.Block() as block:
            @block.gpsimd
            def _(pool):
                def spread(i, s, r):
                    if not first(i, 4):
                        pool.wait_ge(q["rows_ps"], i - 3)
                    pool.tensor_copy(rows[:, s].rearrange("p (h n r) -> p h n r", h=2, r=4),
                                     OUT0[:, :, bass.ds(i, 1), :].broadcast_to([P, 2, S // 4, 4]))\
                        .then_inc(q["rows"], 1)

                def rstd(i, s, r):
                    ln_rstd(pool, q, L, C["minus_half"][:], i, s, 4)

                def rounded(i, s, r):
                    read = [] if first(i, 4) else [(q["turned"], i - 3)]
                    wait_alone(pool, (q["shifted"], i + 1), *read)
                    pool.tensor_scalar(Qb["q16"][:, s], Qb["shifted"][:, s], -ROUND, 0.0, ALU.add, ALU.add)\
                        .then_inc(q["rounded"], 1)

                def add(i, s, r):
                    pool.wait_ge(q["scaled"], i + 1)
                    pool.tensor_tensor(tile_of(X, i), tile_of(X, i), scaled[:, s], ALU.add).then_inc(q["x"], 1)
                stages = [(0, rstd), (1, rounded)]
                if layer == 0:
                    stages = [(0, spread), (1, rstd), (2, rounded), (4, add)]
                pipelined(pool, stages, 4)

            @block.vector
            def _(dve):
                def add_rows(i, s, r):
                    dve.wait_ge(q["rows_ps"], i + 1)
                    dve.tensor_tensor(tile_of(X, i), ps_rows[s % 2], tile_of(X, i), ALU.add).then_inc(q["added"], 1)

                def front(i, s, r):
                    if layer == 0:
                        add_rows(i, s, r)
                    ln_moments(dve, q, L, tile_of(X, i), i, s, (q["added"], i + 1) if layer == 0 else None)

                def norm(i, s, r):
                    ln_xhat(dve, q, L, tile_of(X, i), i, s)
                    dve.wait_ge(q["xhat"], i + 1)
                    quantise(dve, q, Qb, L["xhat"][:, s], floor, i, s)
                    if layer == 1:
                        dve.tensor_tensor(out_scale[:, s:s + 1], Qb["scale"][:, s:s + 1], W["ff1_out"][:], ALU.mult)\
                            .then_inc(q["out_scale"], 1)

                def final(i, s, r):
                    dve.wait_ge(q["y"], i + 1)
                    if layer == 0:
                        if not first(i, 4):
                            dve.wait_ge(q["x"], i - 3)
                        dve.scalar_tensor_tensor(out=scaled[:, s], in0=ps_y[s % 2], scalar=Qb["scale"][:, s:s + 1],
                                                 in1=W["ff0_scale"][:], op0=ALU.mult, op1=ALU.mult)\
                            .then_inc(q["scaled"], 1)
                    else:
                        dve.wait_ge(q["out_scale"], i + 1)
                        dve.scalar_tensor_tensor(out=tile_of(X, i), in0=ps_y[s % 2], scalar=out_scale[:, s:s + 1],
                                                 in1=tile_of(X, i), op0=ALU.mult, op1=ALU.add).then_inc(q["x"], 1)
                pipelined(dve, [(0, front), (1, norm), (3, final)], 4)

            @block.scalar
            def _(act):
                act.preload_act_table(ACT.Exp)

                def keep(i, s, r):
                    act.wait_ge(q["turned"], i + 1)
                    if not first(i, 4):
                        act.wait_ge(q["y"], i - 3)
                    act.activation(qT[:, s], ps_q[s % 2], ACT.Copy).then_inc(q["qT"], 1)

                pipelined(act, [(0, keep)], 4)

            @block.tensor
            def _(pe):
                def rows_out(i, s, r):
                    pe.wait_ge(q["rows"], i + 1)
                    if not first(i, 2):
                        pe.wait_ge(q["added"], i - 1)
                    pe.transpose(ps_rows[s % 2], rows[:, s], C["ident"][:]).then_inc(q["rows_ps"], 1)

                def turned(i, s, r):
                    pe.wait_ge(q["rounded"], i + 1)
                    if not first(i, 2):
                        pe.wait_ge(q["qT"], i - 1)
                    pe.transpose(ps_q[s % 2], Qb["q16"][:, s], C["ident16"][:]).then_inc(q["turned"], 1)

                def product(i, s, r):
                    pe.wait_ge(q["qT"], i + 1)
                    if not first(i, 2):
                        pe.wait_ge(q["scaled" if layer == 0 else "x"], i - 1)
                    pe.matmul(ps_y[s % 2], qT[:, s], w16[:], start=True, stop=True).then_inc(q["y"], 1)
                if layer == 0:
                    pipelined(pe, [(0, rows_out), (2, turned), (3, product)], 4)
                else:
                    pipelined(pe, [(0, turned), (1, product)], 4)



def prepare_attention(k, A, C, layer):
    nc = k.nc
    W = {n: k.sb(f"w{layer}_{n}", [P, D]) for n in ("q", "k", "v", "o", "bias")}
    W["bq"], W["bk"] = k.sb(f"w{layer}_bq", [P, 1]), k.sb(f"w{layer}_bk", [P, 1])
    gate = C["gates"][:, layer:layer + 1]
    with k.scope():
        raw = k.sb(f"pa{layer}_raw", [P, 4, D])
        bv = k.sb(f"pa{layer}_bv", [P, 1])
        bv_wide = k.sb(f"pa{layer}_bv_wide", [P, P])
        bo = k.sb(f"pa{layer}_bo", [P, D])
        loaded = k.sem(f"pa{layer}_loaded")
        with nc.Block() as block:
            @block.sync
            def _(sp):
                for n, m in enumerate("qkvo"):
                    dst = raw[:, n] if layer == 1 else W[m][:]
                    sp.dma_start(dst, A[f"L{layer}_xattn_W{m}"]).then_inc(loaded, 16)
                for dst, m in ((W["bq"], "bq"), (W["bk"], "bk"), (bv, "bv")):
                    sp.dma_start(dst[:], col(A[f"L{layer}_xattn_{m}"])).then_inc(loaded, 16)
                sp.dma_start(bo[:], on_all(A[f"L{layer}_xattn_bo"], D)).then_inc(loaded, 16)
                sp.wait_ge(loaded, 128)
        if layer == 1:
            turn(k, f"pa{layer}_turn", [(W[m][:], raw[:, n]) for n, m in enumerate("qkvo")], C["ident"][:], F32)
        ps = k.psum(f"pa{layer}_bias", [P, D])
        q = k.sems(f"pa{layer}", "wide", "bias_ps", "summed", "scaled")
        with nc.Block() as block:
            @block.vector
            def _(dve):
                dve.tensor_scalar(bv_wide[:], C["ones"][:], bv[:], None, ALU.mult).then_inc(q["wide"], 1)
                dve.wait_ge(q["bias_ps"], 1)
                dve.tensor_tensor(bo[:], ps, bo[:], ALU.add).then_inc(q["summed"], 1)
                dve.wait_ge(q["summed"], 1)
                dve.tensor_scalar(W["bias"][:], bo[:], gate, None, ALU.mult).then_inc(q["scaled"], 1)
                dve.tensor_scalar(W["o"][:], W["o"][:], gate, None, ALU.mult).then_inc(q["scaled"], 1)

            @block.tensor
            def _(pe):
                pe.wait_ge(q["wide"], 1)
                pe.matmul(ps, bv_wide[:], W["o"][:], start=True, stop=True).then_inc(q["bias_ps"], 1)
    return W


def softmax_attention(k, A, C, X, CT, layer):
    nc = k.nc
    W = prepare_attention(k, A, C, layer)
    name = f"at{layer}"
    masked = layer == 1
    NS = 4
    HALF = HEADS // 2
    last = lambda v: min(v, TILES) if isinstance(v, int) else v
    with k.scope():
        L = ln_buffers(k, name, NS)
        ctxT = k.sb(name + "_ctxT", [P, NS, P])
        xT = k.sb(name + "_xT", [P, NS, P])
        qT = k.sb(name + "_qT", [P, NS, P])
        key_wide = k.sb(name + "_key_wide", [P, NS, HALF, P])
        val_wide = k.sb(name + "_val_wide", [P, NS, 2 * HALF, 2, HD + 1])
        probs = k.sb(name + "_probs", [P, NS, HEADS, S])
        top = k.sb(name + "_top", [P, NS, HEADS])
        probs_T = k.sb(name + "_probs_T", [P, NS, HALF, P])
        rsum = k.sb(name + "_rsum", [P, NS, HEADS])
        heads_out = k.sb(name + "_heads_out", [P, NS, D])
        heads_T = k.sb(name + "_heads_T", [P, NS, P])
        if masked:
            causal = k.sb(name + "_causal", [P, S])
            padding = k.sb(name + "_padding", [P, TILES, S], U8)
            bias = k.sb(name + "_mask", [P, NS, S])
            raw = k.sb(name + "_raw", [P, NS, HEADS, S])
        ps_s = k.psum(name + "_scores", [P, HEADS, S])
        ps_t = k.psum(name + "_turned", [P, HALF, P])
        ps_a = k.psum(name + "_a", [P, 2, P])
        ps_q = k.psum(name + "_q", [P, P])
        ps_kv = k.psum(name + "_kv", [P, 2, P])
        ps_o = k.psum(name + "_o", [P, 512])
        pv = ps_o[:, 0:HEADS * (HD + 1)].rearrange("p (h d) -> p h d", h=HEADS)
        out_ps = ps_o[:, 256:256 + D]
        q = k.sems(name, *LN_SEMS, "consts", "ctx_read", "x_turned", "xT", "proj", "qT", "key", "val", "ones",
                   "scores", "mask", "masked", "top", "centred", "exp", "p_turned", "p_kept", "pv", "rsum",
                   "heads", "h_turned", "h_kept", "out", "x", "biased")
        ctx_in = [k.sem(f"{name}_ctx_in{n}") for n in range(NS)]
        with nc.Block() as block:
            @block.sync
            def _(sp):
                if masked:
                    sp.dma_start(causal[:], A["c_causal"]).then_inc(q["consts"], 16)
                    for half in range(2):
                        rows = A["mask_BxS2_bf0"].rearrange("(t b) s -> b t s", b=2)[half:half + 1]
                        sp.dma_start(padding[half * S:(half + 1) * S], rows.broadcast_to([S, TILES, S]))\
                            .then_inc(q["consts"], 16)

                def fetch(i, s, r):
                    if not first(i, NS):
                        sp.wait_ge(q["proj"], i - NS + 1)
                    sp.dma_start(ctxT[:, s], tile_of(CT, i)).then_inc(ctx_in[s], 16)
                pipelined(sp, [(0, fetch)], NS)

            @block.gpsimd
            def _(pool):
                def rstd(i, s, r):
                    ln_rstd(pool, q, L, C["minus_half"][:], i, s, NS)

                def add_bias(i, s, r):
                    pool.wait_ge(q["xhat"], i + 1)
                    pool.tensor_tensor(tile_of(X, i), tile_of(X, i), W["bias"][:], ALU.add).then_inc(q["biased"], 1)

                def centre(i, s, r):
                    pool.wait_ge(q["top"], i + 1)
                    if not first(i, NS):
                        pool.wait_ge(q["p_turned"], i - NS + 1)
                    pool.tensor_tensor(probs[:, s], raw[:, s], top[:, s].unsqueeze(2).broadcast_to([P, HEADS, S]),
                                       ALU.subtract).then_inc(q["centred"], 1)
                stages = [(3, centre)] if masked else []
                pipelined(pool, stages + [(1, add_bias), (0, rstd)], NS)

            @block.vector
            def _(dve):
                for s in range(NS):
                    dve.tensor_copy(val_wide[:, s, :, :, HD], C["half_mask"][:].unsqueeze(1).broadcast_to([P, HEADS, 2]))\
                        .then_inc(q["ones"], 1)
                if masked:
                    dve.wait_ge(q["consts"], 48)

                def final(i, s, r):
                    dve.wait_ge(q["out"], i + 1)
                    dve.wait_ge(q["biased"], i + 1)
                    dve.tensor_tensor(tile_of(X, i), out_ps, tile_of(X, i), ALU.add).then_inc(q["x"], 1)

                def normalise(i, s, r):
                    dve.wait_ge(q["pv"], i + 1)
                    dve.reciprocal(rsum[:, s], pv[:, :, HD]).then_inc(q["rsum"], 1)
                    dve.wait_ge(q["rsum"], i + 1)
                    if not first(i, NS):
                        dve.wait_ge(q["h_turned"], i - NS + 1)
                    dve.tensor_tensor(heads_out[:, s].rearrange("p (h d) -> p h d", h=HEADS), pv[:, :, 0:HD],
                                      rsum[:, s].unsqueeze(2).broadcast_to([P, HEADS, HD]), ALU.mult)\
                        .then_inc(q["heads"], 1)

                def centre(i, s, r):
                    if masked:
                        dve.scalar_tensor_tensor(out=bias[:, s], in0=tile_of(padding, i), scalar=NEG, in1=causal[:],
                                                 op0=ALU.mult, op1=ALU.min).then_inc(q["mask"], 1)
                        dve.wait_ge(q["mask"], i + 1)
                        dve.wait_ge(q["scores"], i + 1)
                        if not first(i, NS):
                            dve.wait_ge(q["centred"], i - NS + 1)
                        dve.tensor_tensor(raw[:, s], ps_s, bias[:, s].unsqueeze(1).broadcast_to([P, HEADS, S]),
                                          ALU.add).then_inc(q["masked"], 1)
                        dve.wait_ge(q["masked"], i + 1)
                        dve.tensor_reduce(top[:, s], raw[:, s], AX.X, ALU.max).then_inc(q["top"], 1)
                    else:
                        dve.wait_ge(q["scores"], i + 1)
                        dve.tensor_reduce(top[:, s], ps_s, AX.X, ALU.max).then_inc(q["top"], 1)
                        dve.wait_ge(q["top"], i + 1)
                        if not first(i, NS):
                            dve.wait_ge(q["p_turned"], i - NS + 1)
                        dve.tensor_tensor(probs[:, s], ps_s, top[:, s].unsqueeze(2).broadcast_to([P, HEADS, S]),
                                          ALU.subtract).then_inc(q["centred"], 1)

                def widen(i, s, r):
                    dve.wait_ge(q["proj"], i + 1)
                    if not first(i, NS):
                        dve.wait_ge(q["scores"], i - NS + 1)
                    dve.scalar_tensor_tensor(out=key_wide[:, s], in0=ps_kv[:, 0].unsqueeze(1).broadcast_to([P, HALF, P]),
                                             scalar=W["bk"][:], in1=C["half_heads"][:].unsqueeze(2).broadcast_to([P, HALF, P]),
                                             op0=ALU.add, op1=ALU.mult).then_inc(q["key"], 1)
                    if not first(i, NS):
                        dve.wait_ge(q["pv"], i - NS + 1)
                    dve.tensor_tensor(val_wide[:, s, :, :, 0:HD],
                                      ps_kv[:, 1].rearrange("p (n d) -> p n d", d=HD).unsqueeze(2).broadcast_to([P, 2 * HALF, 2, HD]),
                                      C["half_mask"][:].unsqueeze(1).unsqueeze(3).broadcast_to([P, 2 * HALF, 2, HD]),
                                      ALU.mult).then_inc(q["val"], 1)

                def norm(i, s, r):
                    ln_xhat(dve, q, L, tile_of(X, i), i, s, q["x_turned"], NS)

                def front(i, s, r):
                    ln_moments(dve, q, L, tile_of(X, i), i, s, None)
                pipelined(dve, [(7, final), (5, normalise), (3, centre), (2, widen), (1, norm), (0, front)], NS)

            @block.scalar
            def _(act):
                act.preload_act_table(ACT.Exp)

                def keep_heads(i, s, r):
                    act.wait_ge(q["h_turned"], i + 1)
                    if not first(i, NS):
                        act.wait_ge(q["out"], i - NS + 1)
                    act.activation(heads_T[:, s], ps_a[:, 1], ACT.Copy).then_inc(q["h_kept"], 1)

                def keep_probs(i, s, r):
                    act.wait_ge(q["p_turned"], i + 1)
                    if not first(i, NS):
                        act.wait_ge(q["pv"], i - NS + 1)
                    act.activation(probs_T[:, s], ps_t, ACT.Copy).then_inc(q["p_kept"], 1)

                def exp(i, s, r):
                    act.wait_ge(q["centred"], i + 1)
                    act.activation(probs[:, s], probs[:, s], ACT.Exp, scale=float(HD) ** -0.5).then_inc(q["exp"], 1)

                def keep_q(i, s, r):
                    act.wait_ge(q["proj"], i + 1)
                    if not first(i, NS):
                        act.wait_ge(q["scores"], i - NS + 1)
                    act.activation(qT[:, s], ps_q, ACT.Identity, bias=W["bq"][:]).then_inc(q["qT"], 1)

                def keep_x(i, s, r):
                    act.wait_ge(q["x_turned"], i + 1)
                    if not first(i, NS):
                        act.wait_ge(q["proj"], i - NS + 1)
                    act.activation(xT[:, s], ps_a[:, 0], ACT.Copy).then_inc(q["xT"], 1)
                pipelined(act, [(6, keep_heads), (4, keep_probs), (3, exp), (2, keep_q), (1, keep_x)], NS)

            @block.tensor
            def _(pe):
                pe.wait_ge(q["ones"], NS)

                def output(i, s, r):
                    pe.wait_ge(q["h_kept"], i + 1)
                    pe.wait_ge(q["heads"], last(i + 2))
                    if isinstance(i, int) and i == TILES - 1:
                        pe.wait_ge(q["x"], i)
                    pe.matmul(out_ps, heads_T[:, s], W["o"][:], start=True, stop=True).then_inc(q["out"], 1)

                def turn_heads(i, s, r):
                    pe.wait_ge(q["heads"], i + 1)
                    pe.wait_ge(q["xT"], last(i + 5))
                    if isinstance(i, int) and i + 5 > TILES:
                        pe.wait_ge(q["h_kept"], i)
                    pe.transpose(ps_a[:, 1], heads_out[:, s], C["ident"][:]).then_inc(q["h_turned"], 1)

                def weigh(i, s, r):
                    pe.wait_ge(q["p_kept"], i + 1)
                    pe.wait_ge(q["val"], i + 1)
                    if not first(i, 2):
                        pe.wait_ge(q["x"], i - 1)
                    elif i == 1:
                        pe.wait_ge(q["heads"], 1)
                    for b in range(2):
                        for j in range(HALF):
                            m = pe.matmul(ps_o[b * S:(b + 1) * S, 2 * j * (HD + 1):2 * (j + 1) * (HD + 1)],
                                          probs_T[:, s, j, b * S:(b + 1) * S],
                                          val_wide[:, s, b * HALF + j].rearrange("p a d -> p (a d)"),
                                          start=True, stop=True)
                    m.then_inc(q["pv"], 1)

                def turn_probs(i, s, r):
                    pe.wait_ge(q["exp"], i + 1)
                    if not first(i, 1):
                        pe.wait_ge(q["p_kept"], i)
                    for j in range(HALF):
                        m = pe.transpose(ps_t[:, j], probs[:, s, 2 * j:2 * j + 2].rearrange("p h k -> p (h k)"), C["ident"][:])
                    m.then_inc(q["p_turned"], 1)

                def scores(i, s, r):
                    read = [] if first(i, 1) else [(q["masked" if masked else "centred"], i)]
                    wait_alone(pe, (q["key"], i + 1), (q["qT"], i + 1), *read)
                    for half in range(2):
                        h = slice(half * S, (half + 1) * S)
                        for b in range(2):
                            t = slice(b * S, (b + 1) * S)
                            m = pe.matmul(ps_s[t, half * HALF:(half + 1) * HALF], qT[h, s, t], key_wide[h, s, :, t],
                                          start=True, stop=True)
                    m.then_inc(q["scores"], 1)

                def project(i, s, r):
                    pe.wait_ge(q["xT"], i + 1)
                    pe.wait_ge(ctx_in[s], 16 * r + 16)
                    if not first(i, 1):
                        pe.wait_ge(q["qT"], i)
                        pe.wait_ge(q["val"], i)
                    pe.matmul(ps_q, W["q"][:], xT[:, s], start=True, stop=True)
                    pe.matmul(ps_kv[:, 0], W["k"][:], ctxT[:, s], start=True, stop=True)
                    for parity in range(2):
                        wv = W["v"][:].rearrange("i (j n d) -> i n j d", n=2, d=HD)[:, parity]
                        for b in range(2):
                            m = pe.matmul(ps_kv[parity * S:(parity + 1) * S, 1, b * S:(b + 1) * S],
                                          ctxT[:, s, b * S:(b + 1) * S], wv, start=True, stop=True)
                    m.then_inc(q["proj"], 1)

                def turn_x(i, s, r):
                    pe.wait_ge(q["xhat"], i + 1)
                    if not first(i, 1):
                        pe.wait_ge(q["xT"], i)
                    if not first(i, 5):
                        pe.wait_ge(q["h_kept"], i - 4)
                    pe.transpose(ps_a[:, 0], L["xhat"][:, s], C["ident"][:]).then_inc(q["x_turned"], 1)
                pipelined(pe, [(7, output), (6, turn_heads), (5, weigh), (4, turn_probs), (3, scores),
                               (2, project), (1, turn_x)], NS)



def retention(k, A, C, X):
    nc = k.nc
    NS = 4
    HALF = HEADS // 2
    with k.scope():
        L = ln_buffers(k, "re", NS)
        rot = k.sb("re_rot", [P, 4, D])
        decay = k.sb("re_decay", [P, HEADS, S])
        ctx = k.sb("re_ctx", [P, NS, D])
        part = k.sb("re_part", [P, NS, 4, D])
        qr = k.sb("re_qr", [P, NS, D])
        kr = k.sb("re_kr", [P, NS, D])
        q_wide = k.sb("re_q_wide", [P, NS, HALF, P])
        kT = k.sb("re_kT", [P, NS, P])
        probs = k.sb("re_probs", [P, NS, HEADS, S])
        ps_q = k.psum("re_q", [P, P])
        ps_k = k.psum("re_k", [P, P])
        ps_s = [k.psum(f"re_s{n}", [P, HEADS, S]) for n in range(2)]
        ps_o = [k.psum(f"re_o{n}", [P, D]) for n in range(2)]
        q = k.sems("re", *LN_SEMS, "consts", "q_cos", "q_sin", "qr", "k_cos", "k_sin", "kr", "q_turned",
                   "k_turned", "q_wide", "kT", "scores", "probs", "out", "x")
        ctx_in = [k.sem(f"re_ctx_in{n}") for n in range(NS)]

        def swapped(eng, out, src, table):
            pairs = lambda ap: ap.rearrange("p (n two) -> p n two", two=2)
            o, x, t = pairs(out), pairs(src), pairs(table)
            yield eng.tensor_tensor(o[:, :, 0], x[:, :, 1], t[:, :, 0], ALU.mult)
            yield eng.tensor_tensor(o[:, :, 1], x[:, :, 0], t[:, :, 1], ALU.mult)

        with nc.Block() as block:
            @block.sync
            def _(sp):
                sp.dma_start(rot[:], A["c_rot"].rearrange("p (n d) -> p n d", n=4)).then_inc(q["consts"], 16)
                sp.dma_start(decay[:], A["c_decay"].rearrange("p (h s) -> p h s", h=HEADS)).then_inc(q["consts"], 16)

                def fetch(i, s, r):
                    if not first(i, NS):
                        sp.wait_ge(q["out"], i - NS + 1)
                    sp.dma_start(ctx[:, s], A["ctx_tiles"][bass.ds(i, 1)].rearrange("a p d -> (a p) d"))\
                        .then_inc(ctx_in[s], 16)
                pipelined(sp, [(0, fetch)], NS)

            @block.gpsimd
            def _(pool):
                pool.wait_ge(q["consts"], 32)

                def rotate_k(i, s, r):
                    pool.wait_ge(ctx_in[s], 16 * r + 16)
                    if not first(i, NS):
                        pool.wait_ge(q["kr"], i - NS + 1)
                    pool.tensor_tensor(part[:, s, 2], ctx[:, s], rot[:, 2], ALU.mult).then_inc(q["k_cos"], 1)
                    for ins in swapped(pool, part[:, s, 3], ctx[:, s], rot[:, 3]):
                        ins.then_inc(q["k_sin"], 1)
                    pool.wait_ge(q["k_cos"], i + 1)
                    pool.wait_ge(q["k_sin"], 2 * i + 2)
                    if not first(i, NS):
                        pool.wait_ge(q["k_turned"], i - NS + 1)
                    pool.tensor_tensor(kr[:, s], part[:, s, 2], part[:, s, 3], ALU.add).then_inc(q["kr"], 1)

                def rstd(i, s, r):
                    ln_rstd(pool, q, L, C["minus_half"][:], i, s, NS)
                pipelined(pool, [(1, rotate_k), (0, rstd)], NS)

            @block.vector
            def _(dve):
                dve.wait_ge(q["consts"], 32)

                def final(i, s, r):
                    dve.wait_ge(q["out"], i + 1)
                    dve.scalar_tensor_tensor(out=tile_of(X, i), in0=ps_o[s % 2], scalar=C["gates"][:, 2:3],
                                             in1=tile_of(X, i), op0=ALU.mult, op1=ALU.add).then_inc(q["x"], 1)

                def decays(i, s, r):
                    dve.wait_ge(q["scores"], i + 1)
                    if not first(i, NS):
                        dve.wait_ge(q["out"], i - NS + 1)
                    dve.tensor_tensor(probs[:, s], ps_s[s % 2], decay[:], ALU.mult).then_inc(q["probs"], 1)

                def widen(i, s, r):
                    dve.wait_ge(q["q_turned"], i + 1)
                    if not first(i, NS):
                        dve.wait_ge(q["scores"], i - NS + 1)
                    dve.tensor_tensor(q_wide[:, s], ps_q.unsqueeze(1).broadcast_to([P, HALF, P]),
                                      C["half_heads"][:].unsqueeze(2).broadcast_to([P, HALF, P]), ALU.mult)\
                        .then_inc(q["q_wide"], 1)

                def norm(i, s, r):
                    ln_xhat(dve, q, L, tile_of(X, i), i, s)
                    dve.wait_ge(q["xhat"], i + 1)
                    dve.tensor_tensor(part[:, s, 0], L["xhat"][:, s], rot[:, 0], ALU.mult).then_inc(q["q_cos"], 1)
                    for ins in swapped(dve, part[:, s, 1], L["xhat"][:, s], rot[:, 1]):
                        ins.then_inc(q["q_sin"], 1)
                    dve.wait_ge(q["q_cos"], i + 1)
                    dve.wait_ge(q["q_sin"], 2 * i + 2)
                    if not first(i, NS):
                        dve.wait_ge(q["q_turned"], i - NS + 1)
                    dve.tensor_tensor(qr[:, s], part[:, s, 0], part[:, s, 1], ALU.add).then_inc(q["qr"], 1)

                def front(i, s, r):
                    ln_moments(dve, q, L, tile_of(X, i), i, s, None)
                pipelined(dve, [(5, final), (3, decays), (2, widen), (1, norm), (0, front)], NS)

            @block.scalar
            def _(act):
                act.preload_act_table(ACT.Exp)

                def keep_k(i, s, r):
                    act.wait_ge(q["k_turned"], i + 1)
                    if not first(i, NS):
                        act.wait_ge(q["scores"], i - NS + 1)
                    act.activation(kT[:, s], ps_k, ACT.Copy).then_inc(q["kT"], 1)
                pipelined(act, [(2, keep_k)], NS)

            @block.tensor
            def _(pe):
                def weigh(i, s, r):
                    read = [] if first(i, 2) else [(q["x"], i - 1)]
                    wait_alone(pe, (q["probs"], i + 1), (ctx_in[s], 16 * r + 16), *read)
                    for h in range(HEADS):
                        for b in range(2):
                            t = slice(b * S, (b + 1) * S)
                            m = pe.matmul(ps_o[s % 2][t, h * HD:(h + 1) * HD], probs[t, s, h],
                                          ctx[t, s, h * HD:(h + 1) * HD], start=True, stop=True)
                    m.then_inc(q["out"], 1)

                def scores(i, s, r):
                    read = [] if first(i, 2) else [(q["probs"], i - 1)]
                    wait_alone(pe, (q["q_wide"], i + 1), (q["kT"], i + 1), *read)
                    for half in range(2):
                        h = slice(half * S, (half + 1) * S)
                        for b in range(2):
                            t = slice(b * S, (b + 1) * S)
                            m = pe.matmul(ps_s[s % 2][t, half * HALF:(half + 1) * HALF], kT[h, s, t],
                                          q_wide[h, s, :, t], start=True, stop=True)
                    m.then_inc(q["scores"], 1)

                def turns(i, s, r):
                    pe.wait_ge(q["qr"], i + 1)
                    if not first(i, 1):
                        pe.wait_ge(q["q_wide"], i)
                    pe.transpose(ps_q, qr[:, s], C["ident"][:]).then_inc(q["q_turned"], 1)
                    pe.wait_ge(q["kr"], i + 1)
                    if not first(i, 1):
                        pe.wait_ge(q["kT"], i)
                    pe.transpose(ps_k, kr[:, s], C["ident"][:]).then_inc(q["k_turned"], 1)
                pipelined(pe, [(4, weigh), (3, scores), (2, turns)], NS)



def feed_forward_gated(k, A, C, W, X):
    nc = k.nc
    NS = 4
    with k.scope():
        L = ln_buffers(k, "gf", NS)
        Qx = quantise_buffers(k, "gf_x", P)
        Qh = quantise_buffers(k, "gf_h", INNER)
        xT = k.sb("gf_xT", [P, NS, P], BF16)
        hT = k.sb("gf_hT", [P, NS, INNER // P, P], BF16)
        factors = k.sb("gf_factors", [P, NS, 4])
        silu = k.sb("gf_silu", [P, NS, INNER])
        hidden = k.sb("gf_hidden", [P, NS, INNER])
        ps_x = k.psum("gf_x", [P, P], BF16)
        ps_h = k.psum("gf_h", [P, INNER // P, P], BF16)
        ps_g = [k.psum(f"gf_g{n}", [P, INNER]) for n in range(2)]
        ps_u = [k.psum(f"gf_u{n}", [P, INNER]) for n in range(2)]
        ps_d = k.psum("gf_d", [P, D])
        hq = {n: k.sem("gf_h_" + n) for n in QUANT_SEMS}
        q = k.sems("gf", *LN_SEMS, *QUANT_SEMS, "factors", "x_turned", "xT", "g", "u", "silu", "hidden", "h_turned",
                   "hT", "down", "down_factor", "x")
        with nc.Block() as block:
            @block.gpsimd
            def _(pool):
                def round_h(i, s, r):
                    read = [] if first(i, 4) else [(q["h_turned"], i - 3)]
                    wait_alone(pool, (hq["shifted"], i + 1), *read)
                    pool.tensor_scalar(Qh["q16"][:, s], Qh["shifted"][:, s], -ROUND, 0.0, ALU.add, ALU.add)\
                        .then_inc(hq["rounded"], 1)

                def round_x(i, s, r):
                    read = [] if first(i, 4) else [(q["x_turned"], i - 3)]
                    wait_alone(pool, (q["shifted"], i + 1), *read)
                    pool.tensor_scalar(Qx["q16"][:, s], Qx["shifted"][:, s], -ROUND, 0.0, ALU.add, ALU.add)\
                        .then_inc(q["rounded"], 1)

                def rstd(i, s, r):
                    ln_rstd(pool, q, L, C["minus_half"][:], i, s, NS)
                pipelined(pool, [(5, round_h), (2, round_x), (0, rstd)], NS)

            @block.vector
            def _(dve):
                def final(i, s, r):
                    dve.wait_ge(q["down"], i + 1)
                    dve.wait_ge(q["down_factor"], i + 1)
                    dve.scalar_tensor_tensor(out=tile_of(X, i), in0=ps_d, scalar=factors[:, s, 2:3],
                                             in1=tile_of(X, i), op0=ALU.mult, op1=ALU.add).then_inc(q["x"], 1)

                def quantise_h(i, s, r):
                    dve.wait_ge(q["silu"], i + 1)
                    dve.wait_ge(q["u"], i + 1)
                    dve.scalar_tensor_tensor(out=hidden[:, s], in0=ps_u[s % 2], scalar=factors[:, s, 1:2],
                                             in1=silu[:, s], op0=ALU.mult, op1=ALU.mult).then_inc(q["hidden"], 1)
                    dve.wait_ge(q["hidden"], i + 1)
                    quantise(dve, hq, Qh, hidden[:, s], (ALU.max, 1e-5), i, s)
                    dve.tensor_tensor(factors[:, s, 2:3], Qh["scale"][:, s:s + 1], W["down_out"][:], ALU.mult)\
                        .then_inc(q["down_factor"], 1)

                def quantise_x(i, s, r):
                    ln_xhat(dve, q, L, tile_of(X, i), i, s)
                    dve.wait_ge(q["xhat"], i + 1)
                    quantise(dve, q, Qx, L["xhat"][:, s], (ALU.max, 1e-5), i, s)
                    dve.tensor_scalar(factors[:, s, 0:2], W["means"][:, 1:3], Qx["scale"][:, s:s + 1], None, ALU.mult)\
                        .then_inc(q["factors"], 1)

                def front(i, s, r):
                    ln_moments(dve, q, L, tile_of(X, i), i, s, None)
                pipelined(dve, [(7, final), (4, quantise_h), (1, quantise_x), (0, front)], NS)

            @block.scalar
            def _(act):
                act.preload_act_table(ACT.Silu)

                def keep_h(i, s, r):
                    act.wait_ge(q["h_turned"], i + 1)
                    if not first(i, NS):
                        act.wait_ge(q["down"], i - NS + 1)
                    act.activation(hT[:, s], ps_h, ACT.Copy).then_inc(q["hT"], 1)

                def gate(i, s, r):
                    act.wait_ge(q["g"], i + 1)
                    act.wait_ge(q["factors"], i + 1)
                    if not first(i, NS):
                        act.wait_ge(q["hidden"], i - NS + 1)
                    act.activation(silu[:, s], ps_g[s % 2], ACT.Silu, scale=factors[:, s, 0:1]).then_inc(q["silu"], 1)

                def keep_x(i, s, r):
                    act.wait_ge(q["x_turned"], i + 1)
                    if not first(i, NS):
                        act.wait_ge(q["u"], i - NS + 1)
                    act.activation(xT[:, s], ps_x, ACT.Copy).then_inc(q["xT"], 1)
                pipelined(act, [(6, keep_h), (4, gate), (2, keep_x)], NS)

            @block.tensor
            def _(pe):
                def down(i, s, r):
                    pe.wait_ge(q["hT"], i + 1)
                    if not first(i, 1):
                        pe.wait_ge(q["x"], i)
                    for n in range(INNER // P):
                        m = pe.matmul(ps_d, hT[:, s, n], W["down"][:, n], start=n == 0, stop=n == INNER // P - 1)
                    m.then_inc(q["down"], 1)

                def turn_h(i, s, r):
                    pe.wait_ge(hq["rounded"], i + 1)
                    if not first(i, 1):
                        pe.wait_ge(q["hT"], i)
                    for n in range(INNER // P):
                        m = pe.transpose(ps_h[:, n], Qh["q16"][:, s, n * P:(n + 1) * P], C["ident16"][:])
                    m.then_inc(q["h_turned"], 1)

                def gate_up(i, s, r):
                    pe.wait_ge(q["xT"], i + 1)
                    if not first(i, 2):
                        pe.wait_ge(q["hidden"], i - 1)
                    pe.matmul(ps_g[s % 2], xT[:, s], W["gate_up"][:, 0:INNER], start=True, stop=True)\
                        .then_inc(q["g"], 1)
                    pe.matmul(ps_u[s % 2], xT[:, s], W["gate_up"][:, INNER:2 * INNER], start=True, stop=True)\
                        .then_inc(q["u"], 1)

                def turn_x(i, s, r):
                    pe.wait_ge(q["rounded"], i + 1)
                    if not first(i, 1):
                        pe.wait_ge(q["xT"], i)
                    pe.transpose(ps_x, Qx["q16"][:, s], C["ident16"][:]).then_inc(q["x_turned"], 1)
                pipelined(pe, [(7, down), (6, turn_h), (3, gate_up), (2, turn_x)], NS)



HALF_E = SE // 2
RANK = 20


def prepare_switch(k, A, C):
    nc = k.nc
    W = {}
    for n in ("v", "o"):
        W[n] = {part: k.sb(f"sw_{n}_{part}", [P, SH, SE, P], F32R) for part in ("high", "low")}
    W["pair"] = k.sb("sw_pair", [P, SH, P])
    W["sel"] = k.sb("sw_sel", [P, P])
    W["route"] = k.sb("sw_route", [P, 2, SH])
    with k.scope():
        raw = k.sb("swp_raw", [P, 2, SH, P])
        sel = k.sb("swp_sel", [P, P])
        staged = k.sb("swp_staged", [P, 3, 2, SE, P])
        rs = k.sb("swp_rs", [P, 1])
        ps = [k.psum(f"swp_pair{n}", [P, 4, P]) for n in range(2)]
        ps_sel = k.psum("swp_sel", [P, P])
        q = k.sems("swp", "small", "pair_ps", "sel_ps", "kept", "high", "low")
        weights_in = [k.sem(f"swp_weights_in{n}") for n in range(SH)]
        with nc.Block() as block:
            @block.sync
            def _(sp):
                for n, m in enumerate(("q_w", "k_w")):
                    sp.dma_start(raw[:, n], A[f"L3_ffn_{m}"].rearrange("(h p) d -> p h d", p=P)).then_inc(q["small"], 16)
                for n, m in enumerate(("sel_v_w", "sel_o_w")):
                    sp.dma_start(sel[n * S:(n + 1) * S], A[f"L3_ffn_{m}"]).then_inc(q["small"], 16)
                sp.dma_start(rs[:], on_all(A["L3_ffn_route_scale"], 1)).then_inc(q["small"], 16)
                for h in range(SH):
                    if h >= 3:
                        sp.wait_ge(q["low"], 2 * (h - 2))
                    for m, n in enumerate(("v", "o")):
                        src = A[f"L3_ffn_{n}_w"][h * SE:(h + 1) * SE].rearrange("e i o -> i e o")
                        sp.dma_start(staged[:, h % 3, m], src).then_inc(weights_in[h], 16)

            @block.tensor
            def _(pe):
                pe.wait_ge(q["small"], 80)
                for h in range(SH):
                    m = pe.matmul(ps[h // 4][:, h % 4], raw[:, 1, h], raw[:, 0, h], start=True, stop=True)
                m.then_inc(q["pair_ps"], 1)
                pe.transpose(ps_sel, sel[:], C["ident"][:]).then_inc(q["sel_ps"], 1)

            @block.scalar
            def _(act):
                act.preload_act_table(ACT.Exp)
                for h in range(SH):
                    act.wait_ge(weights_in[h], 32)
                    for m, n in enumerate(("v", "o")):
                        act.activation(W[n]["high"][:, h], staged[:, h % 3, m], ACT.Copy).then_inc(q["high"], 1)

            @block.vector
            def _(dve):
                dve.wait_ge(q["pair_ps"], 1)
                for n in range(2):
                    dve.tensor_copy(W["pair"][:, 4 * n:4 * n + 4], ps[n]).then_inc(q["kept"], 1)
                dve.wait_ge(q["sel_ps"], 1)
                dve.tensor_copy(W["sel"][:], ps_sel).then_inc(q["kept"], 1)
                ones = C["ones"][:, 0:SH]
                dve.tensor_scalar(W["route"][:, 0], ones, rs[:], None, ALU.mult).then_inc(q["kept"], 1)
                dve.tensor_scalar(W["route"][:, 1], ones, rs[:], C["gates"][:, 7:8], ALU.mult, ALU.mult)\
                    .then_inc(q["kept"], 1)
                for h in range(SH):
                    for m, n in enumerate(("v", "o")):
                        dve.wait_ge(q["high"], 2 * h + m + 1)
                        dve.tensor_tensor(W[n]["low"][:, h], staged[:, h % 3, m], W[n]["high"][:, h].bitcast(F32),
                                          ALU.subtract)\
                            .then_inc(q["low"], 1)
    return W


def unit_before(kind, t, h, back):
    if h >= back:
        return kind, t, h - back
    if kind == "v":
        if not first(t, 2):
            return "o", t - 2, h + SH - back
        return None if t == 0 else ("v", 0, h + SH - back)
    if isinstance(t, int) and t == TILES - 1:
        return "o", t - 1, h + SH - back
    return "v", t + 1, h + SH - back


def switch_attention(k, A, C, x_in, out):
    nc = k.nc
    W = prepare_switch(k, A, C)
    with k.scope():
        L = ln_buffers(k, "sw")
        x = k.sb("sw_x", [P, 2, P])
        x_res = k.sb("sw_x_res", [P, 2, P])
        xT = k.sb("sw_xT", [P, 2, P])
        xT_high = k.sb("sw_xT_high", [P, 2, P], F32R)
        xT_low = k.sb("sw_xT_low", [P, 2, P], F32R)
        uT = k.sb("sw_uT", [P, SH, P])
        probs = k.sb("sw_probs", [P, 2, SH, S])
        probs_T = k.sb("sw_probs_T", [P, SH, S])
        top = k.sb("sw_top", [P, SH])
        rsum = k.sb("sw_rsum", [P, 3, SH])
        ctx_high = k.sb("sw_ctx_high", [P, 2, SH, 2, S], F32R)
        ctx_low = k.sb("sw_ctx_low", [P, 2, SH, 2, S], F32R)
        scaled = k.sb("sw_scaled", [P, 4, HALF_E, P])
        v_part = k.sb("sw_v_part", [P, SH, 2, P])
        v_pair = k.sb("sw_v_pair", [P, 2, 2, P])
        v = k.sb("sw_v", [P, SH, P])
        o_part = k.sb("sw_o_part", [P, 2, 2, P])
        o_rest = k.sb("sw_o_rest", [P, HALF_E, P])
        o_pair = k.sb("sw_o_pair", [P, 2, 2, P])
        y = k.sb("sw_y", [P, 2, P])
        zeros = k.sb("sw_zeros", [P, P])
        place = k.sb("sw_place", [P, 2 * SH, SE])
        G = [P, 2 * SH, SE]
        decays = k.sb("sw_exp", G)
        r = {n: k.sb("sw_r_" + n, G) for n in ("plus", "p", "eq1", "w1", "sel1", "p2", "eq2", "w2", "sel2", "sel")}
        rm = {n: k.sb("sw_m_" + n, [P, 2 * SH]) for n in ("m1", "w1", "m2", "w2", "sum", "clip", "inv")}
        chosen = k.sb("sw_chosen", [P, 2, 2 * SH, SE])
        norm16 = k.sb("sw_norm", [P, 2, 2 * SH])
        gate_v = k.sb("sw_gate_v", [P, 2, SH, SE])
        gate_o = k.sb("sw_gate_o", [P, 2, SH, SE])
        ps_d = [k.psum(f"sw_d{n}", [P, HALF_E, P]) for n in range(2)]
        ps_a = [k.psum(f"sw_a{n}", [P, HALF_E, P]) for n in range(2)]
        ps_w = [k.psum(f"sw_w{n}", [P, 512]) for n in range(2)]
        ps_s = k.psum("sw_s", [P, SH, S])
        ps_m = k.psum("sw_m", [P, 2, P])
        q = k.sems("sw", *LN_SEMS, "place", "zeros", "x_turned", "xT", "xT_high", "xT_low", "logits", "decays",
                   "ranked", "u", "uT", "scores", "top", "centred", "exp", "p_turned", "p_kept", "rsum",
                   "ctx", "ctx_high", "ctx_low", "v", "v_paired", "o_first", "o_added", "o_paired", "y")
        made = {n: k.sem("sw_made_" + n) for n in "vo"}
        d_mixed = {n: k.sem("sw_d_mixed_" + n) for n in "vo"}
        a_scaled = {n: k.sem("sw_a_scaled_" + n) for n in "vo"}
        pooled = {n: k.sem("sw_pooled_" + n) for n in "vo"}
        x_loaded = [k.sem(f"sw_x_loaded{n}") for n in range(2)]
        res_loaded = [k.sem(f"sw_res_loaded{n}") for n in range(2)]
        stored = [k.sem(f"sw_stored{n}") for n in range(2)]

        with nc.Block() as block:
            @block.sync
            def _(sp):
                sp.dma_start(place[:], A["c_place"].rearrange("p (g e) -> p g e", e=SE)).then_inc(q["place"], 16)

                def tile_in(dst, i):
                    return sp.dma_start(dst, x_in[bass.ds(i, 1)].rearrange("a p d -> (a p) d"))

                def fetch(i, s, rd):
                    if not first(i, 2):
                        sp.wait_ge(q["xhat"], i - 1)
                    tile_in(x[:, s], i).then_inc(x_loaded[s], 16)

                def fetch_residual(i, s, rd):
                    if not first(i, 2):
                        sp.wait_ge(d_mixed["o"], 32 * (i - 2) + 1)
                    tile_in(x_res[:, s], i).then_inc(res_loaded[s], 16)

                def store(i, s, rd):
                    sp.wait_ge(q["y"], i + 1)
                    sp.dma_start(out[bass.ds(i, 1)].rearrange("a p d -> (a p) d"), y[:, s]).then_inc(stored[s], 16)
                pipelined(sp, [(0, fetch), (1, fetch_residual), (3, store)])
                for s in range(2):
                    sp.wait_ge(stored[s], 16 * TILES // 2)

            @block.gpsimd
            def _(pool):
                def rstd(i, s, rd):
                    ln_rstd(pool, q, L, C["minus_half"][:], i, s)

                def low_x(i, s, rd):
                    pool.wait_ge(q["xT_high"], i + 1)
                    if not first(i, 2):
                        pool.wait_ge(made["v"], SH * (i - 1))
                    pool.tensor_tensor(xT_low[:, s], xT[:, s], xT_high[:, s].bitcast(F32), ALU.subtract)\
                        .then_inc(q["xT_low"], 1)

                def add_v(h):
                    def step(i, s, rd):
                        u = SH * i + h
                        pool.wait_ge(a_scaled["v"], 4 * u + 4)
                        pool.wait_ge(d_mixed["v"], 4 * u + 4)
                        pool.tensor_tensor(v_pair[:, h % 2], v_part[:, h], scaled[:, h % 4, 2:4], ALU.add)\
                            .then_inc(pooled["v"], 1)
                        pool.wait_ge(pooled["v"], u + 1)
                        if h == 0 and not first(i, 1):
                            pool.wait_ge(q["ctx"], 2 * i)
                        pool.tensor_tensor(v[:, h], v_pair[:, h % 2, 0], v_pair[:, h % 2, 1], ALU.add).then_inc(q["v"], 1)
                    return step

                def add_o(h):
                    def step(i, s, rd):
                        if h == 0:
                            return
                        u = SH * i + h
                        pool.wait_ge(a_scaled["o"], 4 * u + 4)
                        if h == 1:
                            if not first(i, 1):
                                pool.wait_ge(q["o_paired"], 2 * i)
                            pool.tensor_tensor(o_rest[:], scaled[:, 0], scaled[:, 1], ALU.add).then_inc(pooled["o"], 2)
                        else:
                            pool.wait_ge(pooled["o"], u)
                            pool.tensor_tensor(o_rest[:], o_rest[:], scaled[:, h % 4], ALU.add).then_inc(pooled["o"], 1)
                    return step

                def finish(i, s, rd):
                    pool.wait_ge(pooled["o"], SH * i + SH)
                    pool.wait_ge(d_mixed["o"], 32 * i + 32)
                    pool.tensor_tensor(o_pair[:, 0], o_rest[:, 0:2], o_rest[:, 2:4], ALU.add).then_inc(q["o_paired"], 1)
                    pool.wait_ge(q["o_paired"], 2 * i + 1)
                    pool.tensor_tensor(o_pair[:, 1], o_pair[:, 0], o_part[:, s], ALU.add).then_inc(q["o_paired"], 1)
                    pool.wait_ge(q["o_paired"], 2 * i + 2)
                    if not first(i, 2):
                        pool.wait_ge(stored[s], 16 * rd)
                    pool.tensor_tensor(y[:, s], o_pair[:, 1, 0], o_pair[:, 1, 1], ALU.add).then_inc(q["y"], 1)
                stages = [(0, rstd)] + [(1, add_v(h)) for h in range(4)] + [(0, low_x)]
                stages += [(1, add_v(h)) for h in range(4, SH)] + [(2, add_o(h)) for h in range(SH)] + [(2, finish)]
                pipelined(pool, stages)

            @block.scalar
            def _(act):
                act.preload_act_table(ACT.Exp)

                def scale(kind, h):
                    gates = gate_v if kind == "v" else gate_o

                    def step(i, s, rd):
                        u = SH * i + h
                        act.wait_ge(made[kind], u + 1)
                        if h == 0:
                            act.wait_ge(q["ranked"], RANK * i + RANK) if kind == "v" else act.wait_ge(q["rsum"], 4 * i + 4)
                        before = unit_before(kind, i, h, 4)
                        if before is not None:
                            act.wait_ge(pooled[before[0]], SH * before[1] + before[2] + 1)
                        for e in range(HALF_E):
                            act.activation(scaled[:, h % 4, e], ps_a[h % 2][:, e], ACT.Copy,
                                           scale=gates[:, s, h, HALF_E + e:HALF_E + e + 1]).then_inc(a_scaled[kind], 1)
                    return step

                def keep_x(i, s, rd):
                    act.wait_ge(q["x_turned"], i + 1)
                    if not first(i, 2):
                        act.wait_ge(q["scores"], i - 1)
                        act.wait_ge(q["xT_low"], i - 1)
                        act.wait_ge(made["v"], SH * (i - 1))
                    act.activation(xT[:, s], ps_m[:, 0], ACT.Copy).then_inc(q["xT"], 1)
                    act.activation(xT_high[:, s], ps_m[:, 0], ACT.Copy).then_inc(q["xT_high"], 1)

                def keep_probs(i, s, rd):
                    act.wait_ge(q["p_turned"], i + 1)
                    if not first(i, 1):
                        act.wait_ge(q["ctx"], 2 * i)
                    act.activation(probs_T[:], ps_s, ACT.Copy).then_inc(q["p_kept"], 1)

                def exp_logits(i, s, rd):
                    act.wait_ge(q["logits"], i + 1)
                    if not first(i, 1):
                        act.wait_ge(q["ranked"], RANK * i)
                    act.activation(decays[:], ps_m[:, 1].rearrange("p (g e) -> p g e", e=SE), ACT.Exp, scale=-1.0)\
                        .then_inc(q["decays"], 1)

                def keep_u(i, s, rd):
                    for n in range(2):
                        act.wait_ge(q["u"], 2 * i + n + 1)
                        if n == 0 and not first(i, 1):
                            act.wait_ge(q["scores"], i)
                        act.activation(uT[:, 4 * n:4 * n + 4], ps_w[n].rearrange("p (h t) -> p h t", h=4), ACT.Copy)\
                            .then_inc(q["uT"], 1)

                def keep_ctx(i, s, rd):
                    for b in range(2):
                        act.wait_ge(q["ctx"], 2 * i + b + 1)
                        if b == 0 and not first(i, 2):
                            act.wait_ge(made["o"], SH * (i - 1))
                        act.activation(ctx_high[:, s, :, b], ps_w[b].rearrange("p (h t) -> p h t", h=SH), ACT.Copy)\
                            .then_inc(q["ctx_high"], 1)

                def exp_scores(i, s, rd):
                    act.wait_ge(q["centred"], i + 1)
                    act.activation(probs[:, s], probs[:, s], ACT.Exp, scale=float(P) ** -0.5).then_inc(q["exp"], 1)
                stages = [(1, scale("v", h)) for h in range(4)] + [(0, keep_x)]
                stages += [(1, scale("v", h)) for h in range(4, SH)]
                stages += [(1, keep_probs), (0, exp_logits), (0, keep_u), (1, keep_ctx)]
                stages += [(2, scale("o", h)) for h in range(4)] + [(0, exp_scores)]
                stages += [(2, scale("o", h)) for h in range(4, SH)]
                pipelined(act, stages)

            @block.vector
            def _(dve):
                dve.memset(zeros[:], 0.0).then_inc(q["zeros"], 1)
                dve.wait_ge(q["zeros"], 1)
                dve.wait_ge(q["place"], 16)

                def wide(ap):
                    return ap.unsqueeze(2).broadcast_to([P, 2 * SH, SE])

                def front(i, s, rd):
                    ln_moments(dve, q, L, x[:, s], i, s, (x_loaded[s], 16 * rd + 16))

                def norm(i, s, rd):
                    ln_xhat(dve, q, L, x[:, s], i, s, q["x_turned"])

                def sums(i, s, rd):
                    dve.wait_ge(q["exp"], i + 1)
                    dve.tensor_reduce(rsum[:, 0], probs[:, s], AX.X, ALU.add).then_inc(q["rsum"], 1)
                    dve.wait_ge(q["rsum"], 4 * i + 1)
                    dve.reciprocal(rsum[:, 1], rsum[:, 0]).then_inc(q["rsum"], 1)
                    dve.wait_ge(q["rsum"], 4 * i + 2)
                    dve.tensor_tensor(rsum[:, 2], rsum[:, 1], norm16[:, s, SH:], ALU.mult).then_inc(q["rsum"], 1)
                    dve.wait_ge(q["rsum"], 4 * i + 3)
                    dve.tensor_tensor(gate_o[:, s], chosen[:, s, SH:], rsum[:, 2].unsqueeze(2).broadcast_to([P, SH, SE]),
                                      ALU.mult).then_inc(q["rsum"], 1)

                def mix(kind, h):
                    gates = gate_v if kind == "v" else gate_o

                    def step(i, s, rd):
                        u = SH * i + h
                        acc = v_part[:, h] if kind == "v" else o_part[:, s]
                        dve.wait_ge(made[kind], u + 1)
                        if kind == "v":
                            dve.wait_ge(a_scaled["v"], 4 * u + 2)
                            if h == 0:
                                dve.wait_ge(q["ranked"], RANK * i + RANK)
                        elif h == 0:
                            dve.wait_ge(res_loaded[s], 16 * rd + 16)
                            dve.wait_ge(q["rsum"], 4 * i + 4)
                            if not first(i, 2):
                                dve.wait_ge(q["o_paired"], 2 * (i - 1))
                        for e in range(HALF_E):
                            if kind == "v":
                                before = scaled[:, h % 4, e] if e < 2 else acc[:, e % 2]
                            else:
                                before = acc[:, e % 2] if h or e >= 2 else (x_res[:, s] if e == 0 else zeros[:])
                            if e >= 2 or (kind == "o" and h):
                                dve.wait_ge(d_mixed[kind], 4 * u + e - 1)
                            dve.scalar_tensor_tensor(out=acc[:, e % 2], in0=ps_d[h % 2][:, e], scalar=gates[:, s, h, e:e + 1],
                                                     in1=before, op0=ALU.mult, op1=ALU.add).then_inc(d_mixed[kind], 1)
                    return step

                def route(lo, hi):
                    def step(i, s, rd):
                        ops = [
                            lambda: dve.tensor_scalar(r["plus"][:], decays[:], 1.0, None, ALU.add),
                            lambda: dve.reciprocal(r["p"][:], r["plus"][:]),
                            lambda: dve.tensor_reduce(rm["m1"][:], r["p"][:], AX.X, ALU.max),
                            lambda: dve.tensor_tensor(r["eq1"][:], r["p"][:], wide(rm["m1"][:]), ALU.is_equal),
                            lambda: dve.tensor_tensor(r["w1"][:], r["eq1"][:], place[:], ALU.mult),
                            lambda: dve.tensor_reduce(rm["w1"][:], r["w1"][:], AX.X, ALU.max),
                            lambda: dve.tensor_tensor(r["sel1"][:], r["w1"][:], wide(rm["w1"][:]), ALU.is_equal),
                            lambda: dve.scalar_tensor_tensor(out=r["p2"][:], in0=r["sel1"][:], scalar=-2.0, in1=r["p"][:],
                                                             op0=ALU.mult, op1=ALU.add),
                            lambda: dve.tensor_reduce(rm["m2"][:], r["p2"][:], AX.X, ALU.max),
                            lambda: dve.tensor_tensor(r["eq2"][:], r["p2"][:], wide(rm["m2"][:]), ALU.is_equal),
                            lambda: dve.tensor_tensor(r["w2"][:], r["eq2"][:], place[:], ALU.mult),
                            lambda: dve.tensor_reduce(rm["w2"][:], r["w2"][:], AX.X, ALU.max),
                            lambda: dve.tensor_tensor(r["sel2"][:], r["w2"][:], wide(rm["w2"][:]), ALU.is_equal),
                            lambda: dve.tensor_tensor(r["sel"][:], r["sel1"][:], r["sel2"][:], ALU.add),
                            lambda: dve.tensor_tensor(chosen[:, s], r["p"][:], r["sel"][:], ALU.mult),
                            lambda: dve.tensor_tensor(rm["sum"][:], rm["m1"][:], rm["m2"][:], ALU.add),
                            lambda: dve.tensor_scalar(rm["clip"][:], rm["sum"][:], 1e-9, None, ALU.max),
                            lambda: dve.reciprocal(rm["inv"][:], rm["clip"][:]),
                            lambda: dve.tensor_tensor(norm16[:, s], rm["inv"][:], W["route"][:].rearrange("p k h -> p (k h)"),
                                                      ALU.mult),
                            lambda: dve.tensor_tensor(gate_v[:, s], chosen[:, s, 0:SH],
                                                      norm16[:, s, 0:SH].unsqueeze(2).broadcast_to([P, SH, SE]), ALU.mult),
                        ]
                        assert len(ops) == RANK
                        for n in range(lo, hi):
                            if n == 0:
                                dve.wait_ge(q["decays"], i + 1)
                            else:
                                dve.wait_ge(q["ranked"], RANK * i + n)
                            if n == RANK - 1 and not first(i, 2):
                                dve.wait_ge(a_scaled["v"], 32 * (i - 1))
                            ops[n]().then_inc(q["ranked"], 1)
                    return step

                def low_ctx(i, s, rd):
                    for b in range(2):
                        dve.wait_ge(q["ctx_high"], 2 * i + b + 1)
                        dve.tensor_tensor(ctx_low[:, s, :, b], ps_w[b].rearrange("p (h t) -> p h t", h=SH),
                                          ctx_high[:, s, :, b].bitcast(F32), ALU.subtract).then_inc(q["ctx_low"], 1)

                def centre(i, s, rd):
                    dve.wait_ge(q["scores"], i + 1)
                    dve.tensor_reduce(top[:], ps_s, AX.X, ALU.max).then_inc(q["top"], 1)
                    dve.wait_ge(q["top"], i + 1)
                    if not first(i, 2):
                        dve.wait_ge(q["p_turned"], i - 1)
                    dve.tensor_tensor(probs[:, s], ps_s, top[:].unsqueeze(2).broadcast_to([P, SH, S]), ALU.subtract)\
                        .then_inc(q["centred"], 1)
                stages = [(0, front), (1, mix("v", 0)), (1, mix("v", 1)), (0, norm), (1, mix("v", 2)), (1, sums)]
                stages += [(1, mix("v", h)) for h in range(3, SH)]
                stages += [(0, route(0, 8)), (1, low_ctx), (2, mix("o", 0)), (0, centre), (2, mix("o", 1))]
                stages += [(0, route(8, 10)), (2, mix("o", 2)), (0, route(10, 12)), (2, mix("o", 3)), (0, route(12, 14)),
                           (2, mix("o", 4)), (0, route(14, 17)), (2, mix("o", 5)), (0, route(17, RANK)),
                           (2, mix("o", 6)), (2, mix("o", 7))]
                pipelined(dve, stages)

            @block.tensor
            def _(pe):
                def unit(kind, h):
                    def step(i, s, rd):
                        waits = []
                        before = unit_before(kind, i, h, 2)
                        if before is not None:
                            n = 4 * (SH * before[1] + before[2] + 1)
                            waits += [(d_mixed[before[0]], n), (a_scaled[before[0]], n)]
                        if h == 0:
                            waits += [(q["xT_low"], i + 1)] if kind == "v" else [(q["ctx_low"], 2 * i + 2)]
                        wait_alone(pe, *waits) if waits else None
                        if kind == "v":
                            lhs = {"high": xT_high[:, s], "low": xT_low[:, s]}
                        else:
                            lhs = {n: c[:, s, h].rearrange("p b t -> p (b t)") for n, c in (("high", ctx_high), ("low", ctx_low))}
                        w = W[kind]
                        for bank, experts in ((ps_a[h % 2], slice(HALF_E, SE)), (ps_d[h % 2], slice(0, HALF_E))):
                            for n, (a, b) in enumerate((("high", "high"), ("high", "low"), ("low", "high"))):
                                m = pe.matmul(bank, lhs[a], w[b][:, h, experts], start=n == 0, stop=n == 2)
                        m.then_inc(made[kind], 1)
                    return step

                def turn_x(i, s, rd):
                    pe.wait_ge(q["xhat"], i + 1)
                    if not first(i, 1):
                        pe.wait_ge(q["decays"], i)
                    pe.transpose(ps_m[:, 0], L["xhat"][:, s], C["ident"][:]).then_inc(q["x_turned"], 1)

                def turn_probs(i, s, rd):
                    wait_alone(pe, (q["exp"], i + 1))
                    for h in range(SH):
                        for b in range(2):
                            t = slice(b * S, (b + 1) * S)
                            m = pe.matmul(ps_s[t, h], probs[t, s, h], C["ident"][t, t], start=True, stop=True)
                    m.then_inc(q["p_turned"], 1)

                def front(i, s, rd):
                    pe.wait_ge(q["xT_high"], i + 1)
                    pe.matmul(ps_m[:, 1], xT[:, s], W["sel"][:], start=True, stop=True).then_inc(q["logits"], 1)
                    for n in range(2):
                        if not first(i, 2):
                            pe.wait_ge(q["ctx_low"], 2 * (i - 2) + n + 1)
                        elif i == 1:
                            pe.wait_ge(q["uT"], 1 + n)
                        for h in range(4):
                            m = pe.matmul(ps_w[n][:, h * P:(h + 1) * P], W["pair"][:, 4 * n + h], xT[:, s],
                                          start=True, stop=True)
                        m.then_inc(q["u"], 1)

                def context(i, s, rd):
                    upto = min(i + 2, TILES) if isinstance(i, int) else i + 2
                    wait_alone(pe, (q["v"], SH * i + SH), (q["p_kept"], i + 1), (q["uT"], 2 * upto))
                    if isinstance(i, int) and i == TILES - 1:
                        pe.wait_ge(q["ctx_low"], 2 * i)
                    for b in range(2):
                        t = slice(b * S, (b + 1) * S)
                        for h in range(SH):
                            m = pe.matmul(ps_w[b][:, h * S:(h + 1) * S], v[t, h], probs_T[t, h], start=True, stop=True)
                        m.then_inc(q["ctx"], 1)

                def scores(i, s, rd):
                    waits = [(q["uT"], 2 * i + 2)]
                    if not first(i, 1):
                        waits.append((q["p_kept"], i))
                    wait_alone(pe, *waits)
                    for b in range(2):
                        t = slice(b * S, (b + 1) * S)
                        m = pe.matmul(ps_s[t], xT[:, s, t], uT[:, :, t], start=True, stop=True)
                    m.then_inc(q["scores"], 1)
                stages = [(1, unit("v", h)) for h in range(4)] + [(0, turn_x)]
                stages += [(1, unit("v", h)) for h in range(4, SH)]
                stages += [(1, turn_probs), (0, front), (1, context), (0, scores)]
                stages += [(2, unit("o", h)) for h in range(SH)]
                pipelined(pe, stages)


def store_x(k, X, out):
    nc = k.nc
    with nc.Block() as block:
        @block.sync
        def _(sp):
            stored = k.sem("x_stored")
            for n in range(0, TILES, 8):
                sp.dma_start(out[n:n + 8].rearrange("a p d -> p a d"), X[:, n:n + 8]).then_inc(stored, 16)
            sp.wait_ge(stored, 16 * TILES // 8)


def program(nc, A, out):
    k = Core(nc)
    C, W = {}, {}
    scratch = {n: nc.dram_tensor("scratch_" + n, [S * 4 * S * 2], F32, kind="Internal") for n in ("lags", "circ")}
    x3 = nc.dram_tensor("scratch_x", [TILES * P * D], F32, kind="Internal").ap()\
        .rearrange("(t p d) -> t p d", p=P, d=D)
    with k.stack:
        build_constants(k, A, C)
        W["C"] = C
        with k.scope():
            X = k.sb("x", [P, TILES, D])
            CT = k.sb("ctx_T", [P, TILES, P])
            prepare_quantised(k, A, W)
            with k.scope():
                V0 = k.sb("v0", [P, TILES, C0])
                OUT0 = k.sb("out0", [P, 2, TILES, 4])
                GT = load_and_correlate(k, A, C, X, CT, V0)
                lag_weights(k, A, C, GT, OUT0, V0, scratch)
                feed_forward_int(k, A, C, W, X, 0, OUT0)
            softmax_attention(k, A, C, X, CT, 1)
            feed_forward_int(k, A, C, W, X, 1, None)
            retention(k, A, C, X)
            feed_forward_gated(k, A, C, W, X)
            softmax_attention(k, A, C, X, CT, 3)
            store_x(k, X, x3)
        switch_attention(k, A, C, x3, out)



def kernel(**inputs):
    import concourse.bacc as bacc
    from concourse.bass_utils import run_bass_kernel_spmd

    nc = bacc.Bacc("TRN2", target_bir_lowering=False, num_devices=1)
    arrays, A = {}, {}
    for name, a in inputs.items():
        a = np.ascontiguousarray(a)
        arrays[name] = a
    for name, a in host_constants().items():
        arrays["c_" + name] = a
    for name, a in arrays.items():
        A[name] = nc.dram_tensor("in_" + name, a.shape, mybir.dt.from_np(a.dtype), kind="ExternalInput").ap()
    A["x_tiles"] = A["x"].rearrange("(t b) s d -> t (b s) d", b=2)
    A["ctx_tiles"] = A["ctx_1024"].rearrange("(t b) s d -> t (b s) d", b=2)
    out = nc.dram_tensor("out", (B, S, D), F32, kind="ExternalOutput").ap()
    program(nc, A, out.rearrange("(t b) s d -> t (b s) d", b=2))
    r = run_bass_kernel_spmd(nc, [{"in_" + n: a for n, a in arrays.items()}], core_ids=[0])
    return r.results[0]["out"]
```
